# Optimizing a Trainium2 kernel written in Bass

```python
import numpy as np
import jax
import jax.numpy as jnp

def _softmax(x, axis=-1):
    return jax.nn.softmax(x, axis=axis)

def _gelu(x):
    return jax.nn.gelu(x, approximate=True)

def _silu(x):
    return jax.nn.silu(x)

def _sigmoid(x):
    return jax.nn.sigmoid(x)

def _layernorm(x, axis=-1, eps=1e-05):
    m = jnp.mean(x, axis=axis, keepdims=True)
    v = jnp.var(x, axis=axis, keepdims=True)
    return (x - m) / jnp.sqrt(v + eps)

def _scatter_add(tgt, idx, src, axis=0):
    return tgt.at[idx].add(src)

def _segment_sum(src, seg, n):
    return jax.ops.segment_sum(src, seg, n)
kernel_name = 'mk_seq_preln_d1_jaxref_r8_a04b74'

def setup_inputs(seed: int=0):
    np.random.seed(seed)
    _w = jnp.asarray

    def _L0_attn_setup():
        import jax, jax.numpy as jnp
        import numpy as np
        D_MODEL = 512
        N_HEADS = 32
        HEAD_DIM = D_MODEL // N_HEADS
        CLIP_QKV = 8.0
        ALIBI_BIAS_MAX = 8.0
        LN_EPS = 1e-05

        def _alibi_slopes(n_heads: int, bias_max: float) -> jnp.ndarray:
            next_pow2 = 2 ** int(np.ceil(np.log2(n_heads)))
            m = np.arange(1, next_pow2 + 1, dtype=np.float32) * (bias_max / next_pow2)
            slopes = 1.0 / np.power(2.0, m)
            if next_pow2 != n_heads:
                slopes = np.concatenate([slopes[1::2], slopes[::2]])[:n_heads]
            return jnp.asarray(slopes)

        def _layer_norm(x, w, b):
            mu = jnp.mean(x, axis=-1, keepdims=True)
            var = jnp.mean(jnp.square(x - mu), axis=-1, keepdims=True)
            return (x - mu) * jax.lax.rsqrt(var + LN_EPS) * w + b
        key = jax.random.key(seed)
        ks = jax.random.split(key, 3)
        B, S = (1, 256)
        hidden_states = jax.random.normal(ks[0], (B, S, D_MODEL), dtype=jnp.float32)
        Wqkv = jax.random.normal(ks[1], (3 * D_MODEL, D_MODEL), dtype=jnp.float32) * 0.02
        Wout = jax.random.normal(ks[2], (D_MODEL, D_MODEL), dtype=jnp.float32) * 0.02
        return {'hidden_states': hidden_states, 'Wqkv': Wqkv, 'q_ln_w': jnp.ones((D_MODEL,), jnp.float32), 'q_ln_b': jnp.zeros((D_MODEL,), jnp.float32), 'k_ln_w': jnp.ones((D_MODEL,), jnp.float32), 'k_ln_b': jnp.zeros((D_MODEL,), jnp.float32), 'Wout': Wout}
    _L0_attn_in = _L0_attn_setup()

    def _L0_ffn_setup():
        import jax, jax.numpy as jnp
        import numpy as np
        K, OUT, IN = (4, 512, 512)
        key = jax.random.key(seed)
        k1, k2, k3 = jax.random.split(key, 3)
        x = jax.random.normal(k1, (4, 256, IN), dtype=jnp.float32)
        bits = jax.random.randint(k2, (K, OUT, IN), 0, 2)
        bases = (2 * bits - 1).astype(jnp.int8)
        alphas = jax.random.uniform(k3, (K, OUT, 1), dtype=jnp.float32)
        return {'x': x, 'bases': bases, 'alphas': alphas}
    _L0_ffn_in = _L0_ffn_setup()
    _d = {'L0_attn_hidden_states': _L0_attn_in['hidden_states'], 'L0_attn_Wqkv': _L0_attn_in['Wqkv'], 'L0_attn_q_ln_w': _L0_attn_in['q_ln_w'], 'L0_attn_q_ln_b': _L0_attn_in['q_ln_b'], 'L0_attn_k_ln_w': _L0_attn_in['k_ln_w'], 'L0_attn_k_ln_b': _L0_attn_in['k_ln_b'], 'L0_attn_Wout': _L0_attn_in['Wout'], 'L0_ffn_bases': _L0_ffn_in['bases'], 'L0_ffn_alphas': _L0_ffn_in['alphas']}
    _x0 = _d['L0_attn_hidden_states']
    _d['L0_attn_hidden_states'] = jax.random.normal(jax.random.fold_in(jax.random.key(seed), 1), (2, 1024, 512), dtype=_x0.dtype)
    del _x0
    return _d

def reference(L0_attn_hidden_states, L0_attn_Wqkv, L0_attn_q_ln_w, L0_attn_q_ln_b, L0_attn_k_ln_w, L0_attn_k_ln_b, L0_attn_Wout, L0_ffn_bases, L0_ffn_alphas):

    def _L0_attn_ref(hidden_states, Wqkv, q_ln_w, q_ln_b, k_ln_w, k_ln_b, Wout):
        import jax, jax.numpy as jnp
        import numpy as np
        D_MODEL = 512
        N_HEADS = 32
        HEAD_DIM = D_MODEL // N_HEADS
        CLIP_QKV = 8.0
        ALIBI_BIAS_MAX = 8.0
        LN_EPS = 1e-05

        def _alibi_slopes(n_heads: int, bias_max: float) -> jnp.ndarray:
            next_pow2 = 2 ** int(np.ceil(np.log2(n_heads)))
            m = np.arange(1, next_pow2 + 1, dtype=np.float32) * (bias_max / next_pow2)
            slopes = 1.0 / np.power(2.0, m)
            if next_pow2 != n_heads:
                slopes = np.concatenate([slopes[1::2], slopes[::2]])[:n_heads]
            return jnp.asarray(slopes)

        def _layer_norm(x, w, b):
            mu = jnp.mean(x, axis=-1, keepdims=True)
            var = jnp.mean(jnp.square(x - mu), axis=-1, keepdims=True)
            return (x - mu) * jax.lax.rsqrt(var + LN_EPS) * w + b
        B, S, _ = hidden_states.shape
        qkv = jnp.einsum('bsd,ed->bse', hidden_states, Wqkv)
        qkv = jnp.clip(qkv, -CLIP_QKV, CLIP_QKV)
        q, k, v = jnp.split(qkv, [D_MODEL, 2 * D_MODEL], axis=-1)
        q = _layer_norm(q, q_ln_w, q_ln_b)
        k = _layer_norm(k, k_ln_w, k_ln_b)
        q = q.reshape(B, S, N_HEADS, HEAD_DIM)
        k = k.reshape(B, S, N_HEADS, HEAD_DIM)
        v = v.reshape(B, S, N_HEADS, HEAD_DIM)
        scale = HEAD_DIM ** (-0.5)
        scores = jnp.einsum('bqhd,bkhd->bhqk', q, k) * scale
        slopes = _alibi_slopes(N_HEADS, ALIBI_BIAS_MAX)
        pos = jnp.arange(S)
        rel = (pos[None, :] - pos[:, None]).astype(jnp.float32)
        scores = scores + slopes[None, :, None, None] * rel[None, None]
        causal = pos[None, :] <= pos[:, None]
        scores = jnp.where(causal[None, None], scores, jnp.float32(-1e+30))
        probs = jax.nn.softmax(scores, axis=-1)
        out = jnp.einsum('bhqk,bkhd->bqhd', probs, v).reshape(B, S, D_MODEL)
        return jnp.einsum('bsd,ed->bse', out, Wout)

    def _L0_ffn_ref(x, bases, alphas):
        import jax, jax.numpy as jnp
        import numpy as np
        K, OUT, IN = (4, 512, 512)
        W_q = jnp.sum(alphas * bases.astype(x.dtype), axis=0)
        return jnp.einsum('bsi,oi->bso', x, W_q)
    x = L0_attn_hidden_states
    x = x + _L0_attn_ref(_layernorm(x, axis=-1), L0_attn_Wqkv, L0_attn_q_ln_w, L0_attn_q_ln_b, L0_attn_k_ln_w, L0_attn_k_ln_b, L0_attn_Wout)
    x = x + _L0_ffn_ref(_layernorm(x, axis=-1), L0_ffn_bases, L0_ffn_alphas)
    return x

_drawn_inputs = setup_inputs


def setup_inputs(seed=0):
    import zlib

    import numpy as np

    out = dict(_drawn_inputs(seed))
    spreads = {'L0_attn_q_ln_w': (1.0, 0.6),
     'L0_attn_q_ln_b': (0.0, 0.8),
     'L0_attn_k_ln_w': (1.0, 0.6),
     'L0_attn_k_ln_b': (0.0, 0.8)}
    factors = {}
    for name, (base, spread) in spreads.items():
        noise = np.random.default_rng([zlib.crc32(name.encode()), seed]).standard_normal(out[name].shape)
        drawn = base * np.exp(spread * noise) if base else spread * noise
        out[name] = jnp.asarray(drawn.astype(out[name].dtype))
    for name, factor in factors.items():
        out[name] = (out[name] * factor).astype(out[name].dtype)
    return out
```

```python
from contextlib import ExitStack

import numpy as np

import concourse.bass as bass
from concourse import mybir

F32 = mybir.dt.float32
F32R = mybir.dt.float32r
BF16 = mybir.dt.bfloat16
ALU = mybir.AluOpType
ACT = mybir.ActivationFunctionType
AX = mybir.AxisListType
ds = bass.ds

P = 128
BANK = 512
D = 512
DC = D // P
BATCH, SEQ = 2, 1024
TILES = BATCH * SEQ // P
TPB = SEQ // P
HEADS, HD = 32, 16
G = 4
GROUPS = BATCH * HEADS // G
GPB = HEADS // G
VW = 32
CLIP = 8.0
EPS = 1e-5
SCALE = HD ** -0.5
ALIBI_MAX = 8.0
MASKED = -1e30

TERMS = [(0, 0), (0, 1), (1, 0), (1, 1), (0, 2), (2, 0)]
MAX_TERMS = 3
BIAS_ROWS = 6
SHIFT_ROWS = 2
EXP_K = len(TERMS) * HD
MAX_K = MAX_TERMS * HD

UNITS = [(h, kb) for h in range(2) for kb in range((h + 1) * TPB // 2)]
NU = len(UNITS)
LAG = 2
AHEAD = 4
P_SLOTS = 3
MAX_RING = 3


def unit_columns(u):
    half, kb = UNITS[u]
    first = max(kb * P, half * BANK)
    return first, (half + 1) * BANK - first


def is_diagonal(u):
    half, kb = UNITS[u]
    return kb * P >= half * BANK




def max_pieces():
    out = []
    for j in range(G):
        for i in range(TPB):
            keys = (i + 1) * P
            if keys > BANK:
                out.append((j, i, 0, BANK, False))
                out.append((j, i, BANK, keys - BANK, True))
            else:
                out.append((j, i, 0, keys, True))
    return out


PIECES = max_pieces()
NP = len(PIECES)
assert NP % MAX_RING == 0 and (2 * NU) % P_SLOTS == 0


def piece_plan():
    cols = [unit_columns((v + NU - AHEAD) % NU)[1] for v in range(NU)]
    work = [n for _, _, _, n, _ in PIECES]
    plan, done, at, target = [], 0, 0, 0
    for v in range(NU):
        target += cols[v] * sum(work) / sum(cols)
        mine = []
        while at < NP and (done < target - 64 or v == NU - 1):
            mine.append(at)
            done += work[at]
            at += 1
        plan.append(mine)
    return plan


PLAN = piece_plan()


def build(nc, x, wqkv_t, qk_w, qk_b, wout_t, bases_t, alphas, bias_rows, out):
    ctx = ExitStack()

    def alloc(stack):
        def sb(name, shape, dt=F32):
            return stack.enter_context(nc.sbuf_tensor(name, shape, dt))
        return sb

    def sem(name):
        return ctx.enter_context(nc.semaphore(name))

    parts_dram = nc.dram_tensor("parts_dram", [2, 3, BATCH, D, SEQ], BF16).ap()
    v_dram = nc.dram_tensor("v_dram", [BATCH, GPB, TPB, P, G * VW], F32).ap()
    o_dram = nc.dram_tensor("o_dram", [BATCH * HEADS * VW, SEQ], F32).ap()
    inv_dram = nc.dram_tensor("inv_dram", [BATCH, HEADS, SEQ], F32).ap()

    with ctx:
        sb = alloc(ctx)
        ident = sb("ident", [P, P])
        ident_half = sb("ident_half", [P, P], BF16)
        mask = sb("mask", [P, BANK], BF16)
        mask_turned = sb("mask_turned", [P, P], BF16)
        eps = sb("eps", [P, 1])
        wout_hi = sb("wout_hi", [P, DC, D], F32R)
        wout_lo = sb("wout_lo", [P, DC, D], F32R)
        wffn_hi = sb("wffn_hi", [P, DC, D], F32R)
        wffn_lo = sb("wffn_lo", [P, DC, D], F32R)
        wffn_term = sb("wffn_term", [P, 2, D])

        with ExitStack() as staging:
            sb = alloc(staging)
            wqkv_raw = sb("wqkv_raw", [P, DC, 3 * D])
            wout_raw = sb("wout_raw", [P, DC, D])
            bases_sb = sb("bases_sb", [P, 4, DC, D], BF16)
            alpha_sb = sb("alpha_sb", [P, 4, D])
            wffn_sum = sb("wffn_sum", [P, DC, D])
        sb = alloc(ctx)
        max_q = [sb(f"max_q{i}", [P, G, SEQ], BF16) for i in range(2)]
        max_k = [sb(f"max_k{i}", [P, G, SEQ], BF16) for i in range(2)]
        exp_q = [sb(f"exp_q{i}", [P, G, SEQ], BF16) for i in range(2)]
        exp_k = [sb(f"exp_k{i}", [P, G, SEQ], BF16) for i in range(2)]

        with ExitStack() as first:
            sb = alloc(first)
            wqkv_hi = sb("wqkv_hi", [P, DC, 3 * D], F32R)
            wqkv_lo = sb("wqkv_lo", [P, DC, 3 * D], F32R)
            qk_gain = sb("qk_gain", [P, 2, D])
            qk_bias = sb("qk_bias", [P, 2, D])
            x_in = [sb(f"x_in{i}", [P, D]) for i in range(2)]
            xn = [sb(f"xn{i}", [P, D]) for i in range(2)]
            xt_hi = [sb(f"xt_hi{i}", [P, DC, P], F32R) for i in range(2)]
            xt_lo = [sb(f"xt_lo{i}", [P, DC, P], F32R) for i in range(2)]
            qk = [sb(f"qk{i}", [P, 2, D]) for i in range(2)]
            v_ext = [sb(f"v_ext{i}", [P, HEADS, VW]) for i in range(2)]
            rest = sb("rest", [P, 2, DC, P])
            parts = sb("parts", [P, 3, 2, DC, 2 * P], BF16)
            x_stat = sb("x_stat", [P, 6])
            x_mv = [sb(f"x_mv{i}", [P, 2]) for i in range(2)]
            x_sd = [sb(f"x_sd{i}", [P, 1]) for i in range(2)]
            x_rs = [sb(f"x_rs{i}", [P, 1]) for i in range(2)]
            qk_stat = sb("qk_stat", [P, 2, 6])
            qk_mv = [sb(f"qk_mv{i}", [P, 2, 2]) for i in range(2)]
            qk_sd = [sb(f"qk_sd{i}", [P, 2]) for i in range(2)]
            qk_rs = [sb(f"qk_rs{i}", [P, 2]) for i in range(2)]
        sb = alloc(ctx)
        probs = [sb(f"probs{i}", [P, G, BANK]) for i in range(P_SLOTS)]
        v_sb = [sb(f"v_sb{i}", [P, TPB, G * VW]) for i in range(2)]
        o_sb = [sb(f"o_sb{i}", [P, BANK]) for i in range(2)]
        max_junk = sb("max_junk", [P, MAX_RING, BANK], BF16)
        max_diag = [sb(f"max_diag{i}", [P, G, TPB]) for i in range(2)]
        max_full = [sb(f"max_full{i}", [P, G, TPB // 2]) for i in range(2)]
        shift = [sb(f"shift{i}", [G * TPB, P]) for i in range(2)]
        shift_hi = [sb(f"shift_hi{i}", [G * TPB, P], BF16) for i in range(2)]
        shift_mid = [sb(f"shift_mid{i}", [G * TPB, P], BF16) for i in range(2)]
        o_in = [sb(f"o_in{i}", [P, DC, P]) for i in range(2)]
        inv_in = [sb(f"inv_in{i}", [P, DC, P]) for i in range(2)]
        sums = sb("sums", [P, BATCH, HEADS * SEQ // P])
        inv = sb("inv", [P, BATCH, HEADS * SEQ // P])
        att = [sb(f"att{i}", [P, DC, P]) for i in range(2)]
        att_hi = [sb(f"att_hi{i}", [P, DC, P], F32R) for i in range(2)]
        att_lo = [sb(f"att_lo{i}", [P, DC, P], F32R) for i in range(2)]
        x2 = [sb(f"x2_{i}", [P, D]) for i in range(4)]
        yn = [sb(f"yn{i}", [P, D]) for i in range(2)]
        yt_hi = [sb(f"yt_hi{i}", [P, DC, P], F32R) for i in range(2)]
        yt_lo = [sb(f"yt_lo{i}", [P, DC, P], F32R) for i in range(2)]
        y_out = [sb(f"y_out{i}", [P, D]) for i in range(2)]
        y_stat = sb("y_stat", [P, 6])
        y_mv = [sb(f"y_mv{i}", [P, 2]) for i in range(2)]
        y_sd = [sb(f"y_sd{i}", [P, 1]) for i in range(2)]
        y_rs = [sb(f"y_rs{i}", [P, 1]) for i in range(2)]

        ps = ctx.enter_context(nc.psum_tensor("ps", [P, 8, BANK], F32))
        XT_BANK, QK_BANK, V_BANK, QKT_BANK = 0, (1, 3), 5, 6
        EXP_BANK, PV_BANK, MAX_BANK = (0, 2), 4, 5
        O_BANK, YT_BANK, FF_BANK = (0, 1), (2, 3), (4, 5)

        ident_zero, ident_ready, mask_zero, mask_ready = (
            sem("ident_zero"), sem("ident_ready"), sem("mask_zero"), sem("mask_ready"))
        eps_ready, ones_ready = sem("eps_ready"), sem("ones_ready")
        wqkv_loaded = [sem(f"wqkv_loaded{c}") for c in range(DC)]
        gain_loaded, wout_loaded, bases_loaded, alphas_loaded = (
            sem("gain_loaded"), sem("wout_loaded"), sem("bases_loaded"), sem("alphas_loaded"))
        wqkv_hi_ready, wqkv_ready = sem("wqkv_hi_ready"), sem("wqkv_ready")
        wout_hi_ready, wout_ready = sem("wout_hi_ready"), sem("wout_ready")
        wffn_term_ready, wffn_summed = sem("wffn_term_ready"), sem("wffn_summed")
        wffn_hi_ready, wffn_ready = sem("wffn_hi_ready"), sem("wffn_ready")
        waits_passed = [sem("waits_passed_dve"), sem("waits_passed_pool")]
        x_loaded = [sem(f"x_loaded{i}") for i in range(2)]
        x_stats, x_var, x_dev, x_inv, x_normed = (
            sem("x_stats"), sem("x_var"), sem("x_dev"), sem("x_inv"), sem("x_normed"))
        xt_done, xt_hi_ready, xt_ready = sem("xt_done"), sem("xt_hi_ready"), sem("xt_ready")
        qk_done, v_done = sem("qk_done"), sem("v_done")
        qk_clipped, v_clipped = sem("qk_clipped"), sem("v_clipped")
        qk_stats, qk_var, qk_dev, qk_inv, qk_normed = (
            sem("qk_stats"), sem("qk_var"), sem("qk_dev"), sem("qk_inv"), sem("qk_normed"))
        qk_scaled, qk_ready = sem("qk_scaled"), sem("qk_ready")
        qkt_done, hi_ready, rest_ready, mid_ready, lo_ready = (
            sem("qkt_done"), sem("hi_ready"), sem("rest_ready"), sem("mid_ready"), sem("lo_ready"))
        v_stored = [sem(f"v_stored{i}") for i in range(2)]
        parts_stored = sem("parts_stored")
        max_loaded = [sem(f"max_loaded{i}") for i in range(2)]
        exp_loaded = [sem(f"exp_loaded{i}") for i in range(2)]
        v_loaded = [sem(f"v_loaded{i}") for i in range(2)]
        shift_loaded = [sem(f"shift_loaded{i}") for i in range(2)]
        max_scored, max_taken, max_joined, max_turned = (
            sem("max_scored"), sem("max_taken"), sem("max_joined"), sem("max_turned"))
        shift_hi_ready, shift_ready = sem("shift_hi_ready"), sem("shift_ready")
        scored, exp_done, pv_done, o_ready = (
            sem("scored"), sem("exp_done"), sem("pv_done"), sem("o_ready"))
        o_stored = [sem(f"o_stored{i}") for i in range(2)]
        o_loaded = [sem(f"o_loaded{i}") for i in range(2)]
        xr_loaded = [sem(f"xr_loaded{i}") for i in range(4)]
        sums_loaded, inverted, inv_stored = sem("sums_loaded"), sem("inverted"), sem("inv_stored")
        att_ready, att_hi_ready, att_lo_ready = (
            sem("att_ready"), sem("att_hi_ready"), sem("att_lo_ready"))
        proj_done, x2_ready = sem("proj_done"), sem("x2_ready")
        y_stats, y_var, y_dev, y_inv, y_normed = (
            sem("y_stats"), sem("y_var"), sem("y_dev"), sem("y_inv"), sem("y_normed"))
        yt_done, yt_hi_ready, yt_ready = sem("yt_done"), sem("yt_hi_ready"), sem("yt_ready")
        ff_done, y_ready = sem("ff_done"), sem("y_ready")
        y_stored = [sem(f"y_stored{i}") for i in range(2)]

        block = ctx.enter_context(nc.Block())

        def run(eng, step, first, last, body, loop_first, rounds):
            for s in range(first, loop_first):
                step(s, 0)
            with eng.Fori(0, rounds) as it:
                for s in range(loop_first, loop_first + body):
                    step(s, it)
            for s in range(loop_first + body * rounds, last + 1):
                step(s, 0)

        def wait_apart(eng, semaphore, value):
            eng.wait_ge(semaphore, value)
            eng.sem_inc(waits_passed[eng is nc.gpsimd], 1)

        def run_tiles(eng, step, first, last):
            run(eng, step, first, last, 2, 4, 4)

        def run_units(eng, step):
            run(eng, step, -NU - AHEAD, GROUPS * NU + LAG - 1, 2 * NU, NU + LAG + 1, GROUPS // 2 - 2)

        def run_groups(eng, step):
            run(eng, step, -2, GROUPS, 2, 1, GROUPS // 2 - 2)

        def run_outputs(eng, step):
            run(eng, step, -2, TILES - 1, 4, 2, TILES // 4 - 1)

        @block.sync
        def _(sp):
            sp.dma_start(x_in[0][:], x[0]).then_inc(x_loaded[0], 16)
            for c in range(DC):
                sp.dma_start(wqkv_raw[:, c, :], wqkv_t[c * P:(c + 1) * P, :]).then_inc(wqkv_loaded[c], 16)
            sp.dma_start(x_in[1][:], x[1]).then_inc(x_loaded[1], 16)
            for i in range(2):
                sp.dma_start(qk_gain[:, i, :], qk_w[i:i + 1, :].partition_broadcast(P)).then_inc(gain_loaded, 16)
                sp.dma_start(qk_bias[:, i, :], qk_b[i:i + 1, :].partition_broadcast(P)).then_inc(gain_loaded, 16)
            for k in range(4):
                sp.dma_start(alpha_sb[:, k, :], alphas[k:k + 1, :].partition_broadcast(P)).then_inc(alphas_loaded, 16)
            sp.dma_start(wout_raw[:], wout_t.rearrange("(c p) o -> p c o", p=P)).then_inc(wout_loaded, 16)

            def tile_step(s, it):
                t = s + 3
                if 2 <= t < TILES:
                    sp.wait_ge(x_normed, t - 1 + 2 * it)
                    sp.dma_start(x_in[t % 2][:], x[t + 2 * it]).then_inc(x_loaded[t % 2], 16)
                t = s
                if 0 <= t < TILES:
                    sp.wait_ge(v_clipped, t + 1 + 2 * it)
                    tt = t + 2 * it
                    sp.dma_start(v_dram[tt // TPB, :, tt % TPB, :, :].rearrange("g p n -> p g n"),
                                 v_ext[t % 2][:].rearrange("p (g h) n -> p g (h n)", g=GPB)
                                 ).then_inc(v_stored[t % 2], 16)
                t = s - 2
                if 0 <= t < TILES and t % 2:
                    sp.wait_ge(lo_ready, t + 1 + 2 * it)
                    sp.wait_ge(mid_ready, t + 1 + 2 * it)
                    tt = t - 1 + 2 * it
                    for n in range(3):
                        for i in range(2):
                            sp.dma_start(
                                parts_dram[i, n, tt // TPB, :, ds((tt % TPB) * P, 2 * P)]
                                .rearrange("(c p) t -> p c t", p=P),
                                parts[:, n, i, :, :]).then_inc(parts_stored, 16)

            run_tiles(sp, tile_step, -1, TILES + 1)

            sp.wait_ge(qkt_done, TILES)
            sp.wait_ge(parts_stored, 6 * 16 * TILES // 2)
            for i in range(2):
                sp.wait_ge(v_stored[i], 16 * TILES // 2)
            sp.wait_ge(wqkv_ready, DC)
            sp.wait_ge(wout_ready, DC)
            sp.wait_ge(wffn_ready, DC)

            def stack(dst_q, dst_k, terms, n, it, loaded):
                nn = n + 2 * it
                for i, dst in ((0, dst_q), (1, dst_k)):
                    for r, term in enumerate(terms):
                        src = parts_dram[i, term[i]].rearrange("b f t -> (b f) t")
                        sp.dma_start(dst[r * HD:(r + 1) * HD, :, :],
                                     src[ds(nn * (G * HD), G * HD), :].rearrange("(j d) t -> d j t", j=G)
                                     ).then_inc(loaded, 16)
                    r = len(terms) * HD
                    rows = BIAS_ROWS + (SHIFT_ROWS if i == 1 and len(terms) > MAX_TERMS else 0)
                    sp.dma_start(dst[r:r + rows, :, :],
                                 bias_rows[i, 0:rows, ds((nn % GPB) * G, G), :]).then_inc(loaded, 16)

            def group_step(s, it):
                n = s + 2
                if 0 <= n < GROUPS:
                    if n >= 2:
                        sp.wait_ge(max_scored, NP * (n - 1) + 2 * NP * it)
                    stack(max_q[n % 2], max_k[n % 2], TERMS[:MAX_TERMS], n, it, max_loaded[n % 2])
                n = s + 1
                if 0 <= n < GROUPS:
                    if n >= 2:
                        sp.wait_ge(scored, 2 * NU * (n - 1) + 4 * NU * it)
                    stack(exp_q[n % 2], exp_k[n % 2], TERMS, n, it, exp_loaded[n % 2])
                    if n >= 2:
                        sp.wait_ge(pv_done, NU * (n - 1) + 2 * NU * it)
                    nn = n + 2 * it
                    sp.dma_start(v_sb[n % 2][:], v_dram.rearrange("b g k p n -> (b g) k p n")[nn]
                                 .rearrange("k p n -> p k n")).then_inc(v_loaded[n % 2], 16)
                for n, half in ((s - 1, 1), (s, 0)):
                    if 0 <= n < GROUPS:
                        sp.wait_ge(o_ready, 2 * n + half + 1 + 4 * it)
                        sp.dma_start(o_dram[ds((n + 2 * it) * P, P), half * BANK:(half + 1) * BANK],
                                     o_sb[half][:]).then_inc(o_stored[half], 16)
                n = s + 1
                if 0 <= n < GROUPS:
                    sp.wait_ge(shift_ready, n + 1 + 2 * it)
                    for r, part in ((0, shift_hi), (1, shift_mid)):
                        row = EXP_K + BIAS_ROWS + r
                        sp.dma_start(exp_q[n % 2][row:row + 1, :, :].rearrange("p j t -> p (j t)"),
                                     part[n % 2][:]).then_inc(shift_loaded[n % 2], 16)

                if s == GROUPS - 2:
                    load_sums(0)
                if s == GROUPS - 1:
                    store_inverses(0)

            def load_sums(b):
                for half in range(2):
                    sp.wait_ge(o_stored[half], 16 * (GROUPS if b else GROUPS - 1 - half))
                rows = o_dram.rearrange("(b h r) (q t) -> b h r q t", b=BATCH, r=VW, q=P // HEADS)
                sp.dma_start(sums[:, b, :], rows[b, :, HD, :, :]).then_inc(sums_loaded, 16)

            def store_inverses(b):
                sp.wait_ge(inverted, b + 1)
                sp.dma_start(inv_dram[b].rearrange("h (q t) -> (h q) t", q=P // HEADS),
                             inv[:, b, :]).then_inc(inv_stored, 16)

            run_groups(sp, group_step)
            load_sums(1)
            store_inverses(1)
            sp.wait_ge(inv_stored, 16)

            def output_step(s, it):
                t = s + 4
                if 2 <= t < TILES + 2:
                    t -= 2
                    tt = t + 4 * it
                    if t >= 2:
                        sp.wait_ge(att_ready, t - 1 + 4 * it)
                    src = o_dram.rearrange("(b c h r) t -> b c h r t", b=BATCH, c=DC, r=VW)
                    if s == 1:
                        sp.wait_ge(inv_stored, 16 * BATCH)
                    for c in range(DC):
                        heads = HEADS // DC
                        sp.dma_start(o_in[t % 2][:, c, :],
                                     src[tt // TPB, c, :, 0:HD, ds((tt % TPB) * P, P)]).then_inc(o_loaded[t % 2], 16)
                        one = inv_dram[tt // TPB, c * heads:(c + 1) * heads, ds((tt % TPB) * P, P)]
                        sp.dma_start(inv_in[t % 2][:, c, :],
                                     one.rearrange("h (a t) -> h a t", a=1).broadcast_to([heads, HD, P])
                                     ).then_inc(o_loaded[t % 2], 16)
                    if t >= 4:
                        sp.wait_ge(y_ready, t - 3 + 4 * it)
                    sp.dma_start(x2[t % 4][:], x[tt]).then_inc(xr_loaded[t % 4], 16)
                t = s
                if 0 <= t < TILES:
                    sp.wait_ge(y_ready, t + 1 + 4 * it)
                    sp.dma_start(out[t + 4 * it], y_out[t % 2][:]).then_inc(y_stored[t % 2], 16)

            run_outputs(sp, output_step)
            for i in range(2):
                sp.wait_ge(y_stored[i], 16 * TILES // 2)

        @block.gpsimd
        def _(pool):
            for k in range(4):
                pool.dma_start(bases_sb[:, k, :, :],
                               bases_t[k].rearrange("(c p) o -> p c o", p=P)).then_inc(bases_loaded, 16)
            pool.memset(eps[:], EPS).then_inc(eps_ready, 1)
            pool.memset(ident[:], 0.0).then_inc(ident_zero, 1)
            pool.wait_ge(ident_zero, 1)
            pool.affine_select(out=ident[:], in_=ident[:], compare_op=ALU.not_equal, fill=1.0, base=0,
                               pattern=[[-1, P]], channel_multiplier=1).then_inc(ident_ready, 1)
            pool.memset(ident_half[:], 0.0).then_inc(ident_zero, 1)
            pool.wait_ge(ident_zero, 2)
            pool.affine_select(out=ident_half[:], in_=ident_half[:], compare_op=ALU.not_equal, fill=1.0, base=0,
                               pattern=[[-1, P]], channel_multiplier=1).then_inc(ident_ready, 1)
            pool.memset(mask_turned[:], 0.0).then_inc(mask_zero, 1)
            pool.wait_ge(mask_zero, 1)
            pool.affine_select(out=mask_turned[:], in_=mask_turned[:], compare_op=ALU.is_ge, fill=MASKED, base=0,
                               pattern=[[1, P]], channel_multiplier=-1).then_inc(mask_ready, 1)
            pool.memset(mask[:], 0.0).then_inc(mask_zero, 1)
            pool.wait_ge(mask_zero, 2)
            pool.affine_select(out=mask[:], in_=mask[:], compare_op=ALU.is_ge, fill=MASKED, base=BANK - P,
                               pattern=[[-1, BANK]], channel_multiplier=1).then_inc(mask_ready, 1)
            for i in range(2):
                pool.memset(v_ext[i][:], 1.0).then_inc(ones_ready, 1)

            pool.wait_ge(bases_loaded, 4 * 16)
            pool.wait_ge(alphas_loaded, 4 * 16)
            done = 0
            for c in range(DC):
                for k in range(4):
                    to = wffn_sum[:, c, :] if k == 0 else wffn_term[:, k % 2, :]
                    if k and done:
                        pool.wait_ge(wffn_summed, done)
                    pool.tensor_tensor(to, bases_sb[:, k, c, :], alpha_sb[:, k, :],
                                       ALU.mult).then_inc(wffn_term_ready, 1)
                    if k:
                        pool.wait_ge(wffn_term_ready, 4 * c + k + 1)
                        if done:
                            pool.wait_ge(wffn_summed, done)
                        pool.tensor_tensor(wffn_sum[:, c, :], wffn_sum[:, c, :], wffn_term[:, k % 2, :],
                                           ALU.add).then_inc(wffn_summed, 1)
                        done += 1

            def low_part(lo, whole, hi, hi_ready_, ready):
                for c in range(DC):
                    pool.wait_ge(hi_ready_, c + 1)
                    pool.tensor_tensor(lo[:, c, :], whole[:, c, :], hi[:, c, :].bitcast(F32),
                                       ALU.subtract).then_inc(ready, 1)

            def tile_step(s, it):
                t = s - 2
                if 0 <= t < TILES:
                    pool.wait_ge(mid_ready, t + 1 + 2 * it)
                    half = ds((t % 2) * P, P)
                    pool.tensor_tensor(parts[:, 2, :, :, half], rest[:], parts[:, 1, :, :, half],
                                       ALU.subtract).then_inc(lo_ready, 1)
                t = s
                if 0 <= t < TILES:
                    if t == 0:
                        pool.wait_ge(gain_loaded, 4 * 16)
                    pool.wait_ge(qk_normed, t + 1 + 2 * it)
                    pool.tensor_tensor(qk[t % 2][:], qk[t % 2][:], qk_gain[:], ALU.mult).then_inc(qk_scaled, 1)
                    pool.wait_ge(qk_scaled, t + 1 + 2 * it)
                    pool.tensor_tensor(qk[t % 2][:], qk[t % 2][:], qk_bias[:], ALU.add).then_inc(qk_ready, 1)

            run_tiles(pool, tile_step, 0, TILES + 1)
            low_part(wout_lo, wout_raw, wout_hi, wout_hi_ready, wout_ready)
            low_part(wffn_lo, wffn_sum, wffn_hi, wffn_hi_ready, wffn_ready)

            def unit_step(s, it):
                n = (s + AHEAD) // NU
                if (s + AHEAD) % NU == 0 and 0 <= n < GROUPS:
                    pool.wait_ge(shift_hi_ready, 2 * (n + 1) + 4 * it)
                    pool.tensor_tensor(shift_mid[n % 2][:], shift[n % 2][:], shift_hi[n % 2][:],
                                       ALU.subtract).then_inc(shift_ready, 1)

            run_units(pool, unit_step)

            def output_step(s, it):
                t = s + 2
                if 0 <= t < TILES:
                    pool.wait_ge(o_loaded[t % 2], 8 * 16 * (t // 2 + 1) + 2 * 8 * 16 * it)
                    if t >= 2:
                        pool.wait_ge(att_lo_ready, t - 1 + 4 * it)
                    pool.tensor_tensor(att[t % 2][:], o_in[t % 2][:], inv_in[t % 2][:],
                                       ALU.mult).then_inc(att_ready, 1)
                    pool.wait_ge(att_hi_ready, t + 1 + 4 * it)
                    pool.tensor_tensor(att_lo[t % 2][:], att[t % 2][:], att_hi[t % 2][:].bitcast(F32),
                                       ALU.subtract).then_inc(att_lo_ready, 1)

            run_outputs(pool, output_step)

        @block.scalar
        def _(act):
            for c in range(DC):
                act.wait_ge(wqkv_loaded[c], 16)
                act.activation(wqkv_hi[:, c, :], wqkv_raw[:, c, :], ACT.Copy).then_inc(wqkv_hi_ready, 1)
            act.wait_ge(wout_loaded, 16)
            for c in range(DC):
                act.activation(wout_hi[:, c, :], wout_raw[:, c, :], ACT.Copy).then_inc(wout_hi_ready, 1)
            act.wait_ge(eps_ready, 1)

            def tile_step(s, it):
                t = s + 1
                if 0 <= t < TILES:
                    act.wait_ge(xt_done, t + 1 + 2 * it)
                    if t >= 2:
                        act.wait_ge(v_done, t - 1 + 2 * it)
                    act.activation(xt_hi[t % 2][:].rearrange("p c t -> p (c t)"), ps[:, XT_BANK, :],
                                   ACT.Copy).then_inc(xt_hi_ready, 1)
                t = s - 2
                half = ds((t % 2) * P, P)
                if 0 <= t < TILES:
                    act.wait_ge(qkt_done, t + 1 + 2 * it)
                    if t >= 2:
                        act.wait_ge(parts_stored, 6 * 16 * (t // 2) + 6 * 16 * it)
                    act.activation(parts[:, 0, :, :, half],
                                   ps[:, QKT_BANK:QKT_BANK + 2, :].rearrange("p i (c t) -> p i c t", c=DC),
                                   ACT.Copy).then_inc(hi_ready, 1)
                t = s + 2
                if 0 <= t < TILES:
                    act.wait_ge(x_var, t + 1 + 2 * it)
                    act.activation(x_sd[t % 2][:], x_mv[t % 2][:, 1:2], ACT.Sqrt, bias=eps[:]).then_inc(x_dev, 1)
                t = s - 2
                if 0 <= t < TILES:
                    act.wait_ge(rest_ready, t + 1 + 2 * it)
                    act.activation(parts[:, 1, :, :, half], rest[:], ACT.Copy).then_inc(mid_ready, 1)
                t = s
                if 0 <= t < TILES:
                    act.wait_ge(qk_var, t + 1 + 2 * it)
                    act.activation(qk_sd[t % 2][:], qk_mv[t % 2][:, :, 1], ACT.Sqrt, bias=eps[:]).then_inc(qk_dev, 1)

            run_tiles(act, tile_step, -2, TILES + 1)
            act.wait_ge(wffn_summed, 3 * DC)
            for c in range(DC):
                act.activation(wffn_hi[:, c, :], wffn_sum[:, c, :], ACT.Copy).then_inc(wffn_hi_ready, 1)

            def unit_step(s, it):
                n = (s + AHEAD) // NU
                if (s + AHEAD) % NU == 0 and 0 <= n < GROUPS:
                    act.wait_ge(max_turned, n + 1 + 2 * it)
                    turned = ps[0:G * TPB, MAX_BANK, 0:P]
                    act.activation(shift[n % 2][:], turned, ACT.Copy, scale=-1.0).then_inc(shift_hi_ready, 1)
                    act.activation(shift_hi[n % 2][:], turned, ACT.Copy, scale=-1.0).then_inc(shift_hi_ready, 1)
                u = s % NU
                last = s - LAG - 1
                for pair in range(2):
                    if 0 <= s < GROUPS * NU:
                        n = unit_columns(u)[1]
                        act.wait_ge(scored, 2 * s + pair + 1 + 4 * NU * it)
                        if s >= P_SLOTS and pair == 0:
                            act.wait_ge(pv_done, s - P_SLOTS + 1 + 2 * NU * it)
                        act.activation(probs[s % P_SLOTS][:, 2 * pair:2 * pair + 2, 0:n],
                                       ps[:, EXP_BANK[pair]:EXP_BANK[pair] + 2, 0:n],
                                       ACT.Exp, scale=SCALE).then_inc(exp_done, 1)
                    if pair == 0 and last >= 0 and last % NU in (TPB // 2 - 1, NU - 1):
                        copy_half(last, it)

            def copy_half(u, it):
                half = 0 if u % NU == TPB // 2 - 1 else 1
                n = u // NU
                act.wait_ge(pv_done, u + 1 + 2 * NU * it)
                if n >= 1:
                    act.wait_ge(o_stored[half], 16 * n + 32 * it)
                act.activation(o_sb[half][:], ps[:, PV_BANK, :], ACT.Copy).then_inc(o_ready, 1)

            run_units(act, unit_step)
            copy_half(GROUPS * NU - 1, 0)

            def output_step(s, it):
                t = s + 2
                if 0 <= t < TILES:
                    act.wait_ge(att_ready, t + 1 + 4 * it)
                    if t >= 2:
                        act.wait_ge(proj_done, t - 1 + 4 * it)
                    act.activation(att_hi[t % 2][:], att[t % 2][:], ACT.Copy).then_inc(att_hi_ready, 1)
                if 0 <= t < TILES:
                    act.wait_ge(y_var, t + 1 + 4 * it)
                    act.activation(y_sd[t % 2][:], y_mv[t % 2][:, 1:2], ACT.Sqrt, bias=eps[:]).then_inc(y_dev, 1)
                t = s + 1
                if 0 <= t < TILES:
                    act.wait_ge(yt_done, t + 1 + 4 * it)
                    if t >= 2:
                        act.wait_ge(ff_done, t - 1 + 4 * it)
                    act.activation(yt_hi[t % 2][:].rearrange("p c t -> p (c t)"), ps[:, YT_BANK[t % 2], :],
                                   ACT.Copy).then_inc(yt_hi_ready, 1)

            run_outputs(act, output_step)

        @block.vector
        def _(dve):
            for c in range(DC):
                dve.wait_ge(wqkv_hi_ready, c + 1)
                dve.tensor_tensor(wqkv_lo[:, c, :], wqkv_raw[:, c, :], wqkv_hi[:, c, :].bitcast(F32),
                                  ALU.subtract).then_inc(wqkv_ready, 1)

            def tile_step(s, it):
                t = s + 1
                if 0 <= t < TILES:
                    dve.wait_ge(xt_hi_ready, t + 1 + 2 * it)
                    dve.tensor_tensor(xt_lo[t % 2][:].rearrange("p c t -> p (c t)"), ps[:, XT_BANK, :],
                                      xt_hi[t % 2][:].bitcast(F32).rearrange("p c t -> p (c t)"),
                                      ALU.subtract).then_inc(xt_ready, 1)
                t = s + 2
                if 0 <= t < TILES:
                    dve.wait_ge(x_loaded[t % 2], 16 * (t // 2 + 1) + 16 * it)
                    dve.bn_stats(x_stat[:], x_in[t % 2][:]).then_inc(x_stats, 1)
                    wait_apart(dve, x_stats, t + 1 + 2 * it)
                    dve.bn_aggr(x_mv[t % 2][:], x_stat[:]).then_inc(x_var, 1)
                t = s - 2
                if 0 <= t < TILES:
                    dve.wait_ge(hi_ready, t + 1 + 2 * it)
                    if t >= 1:
                        dve.wait_ge(lo_ready, t + 2 * it)
                    dve.tensor_tensor(rest[:],
                                      ps[:, QKT_BANK:QKT_BANK + 2, :].rearrange("p i (c t) -> p i c t", c=DC),
                                      parts[:, 0, :, :, ds((t % 2) * P, P)],
                                      ALU.subtract).then_inc(rest_ready, 1)
                t = s + 2
                if 0 <= t < TILES:
                    dve.wait_ge(x_dev, t + 1 + 2 * it)
                    dve.reciprocal(x_rs[t % 2][:], x_sd[t % 2][:]).then_inc(x_inv, 1)
                    dve.wait_ge(x_inv, t + 1 + 2 * it)
                    if t >= 2:
                        dve.wait_ge(xt_done, t - 1 + 2 * it)
                    dve.tensor_scalar(xn[t % 2][:], x_in[t % 2][:], x_mv[t % 2][:, 0:1], x_rs[t % 2][:],
                                      ALU.subtract, ALU.mult).then_inc(x_normed, 1)
                t = s
                if 0 <= t < TILES:
                    dve.wait_ge(qk_done, t + 1 + 2 * it)
                    if t >= 2:
                        dve.wait_ge(qkt_done, t - 1 + 2 * it)
                    bank = QK_BANK[t % 2]
                    dve.tensor_scalar(qk[t % 2][:], ps[:, bank:bank + 2, :], CLIP, -CLIP,
                                      ALU.min, ALU.max).then_inc(qk_clipped, 1)
                    dve.wait_ge(qk_clipped, t + 1 + 2 * it)
                    for i in range(2):
                        dve.bn_stats(qk_stat[:, i, :], qk[t % 2][:, i, :]).then_inc(qk_stats, 1)
                    wait_apart(dve, qk_stats, 2 * t + 2 + 4 * it)
                    dve.bn_aggr(qk_mv[t % 2][:, 0, :], qk_stat[:, 0, :])
                    dve.bn_aggr(qk_mv[t % 2][:, 1, :], qk_stat[:, 1, :]).then_inc(qk_var, 1)
                    dve.wait_ge(v_done, t + 1 + 2 * it)
                    if t == 0:
                        dve.wait_ge(ones_ready, 2)
                    if t >= 2:
                        dve.wait_ge(v_stored[t % 2], 16 * (t // 2) + 16 * it)
                    dve.tensor_scalar(v_ext[t % 2][:, :, 0:HD],
                                      ps[:, V_BANK, :].rearrange("p (h d) -> p h d", h=HEADS), CLIP, -CLIP,
                                      ALU.min, ALU.max).then_inc(v_clipped, 1)
                    dve.wait_ge(qk_dev, t + 1 + 2 * it)
                    dve.reciprocal(qk_rs[t % 2][:], qk_sd[t % 2][:]).then_inc(qk_inv, 1)
                    dve.wait_ge(qk_inv, t + 1 + 2 * it)
                    dve.tensor_scalar(qk[t % 2][:, 0, :], qk[t % 2][:, 0, :], qk_mv[t % 2][:, 0, 0:1],
                                      qk_rs[t % 2][:, 0:1], ALU.subtract, ALU.mult)
                    dve.tensor_scalar(qk[t % 2][:, 1, :], qk[t % 2][:, 1, :], qk_mv[t % 2][:, 1, 0:1],
                                      qk_rs[t % 2][:, 1:2], ALU.subtract, ALU.mult).then_inc(qk_normed, 1)

            run_tiles(dve, tile_step, -2, TILES + 1)
            dve.wait_ge(mask_ready, 2)

            def unit_step(s, it):
                n = (s + AHEAD) // NU
                if (s + AHEAD) % NU == 0 and 0 <= n < GROUPS:
                    dve.wait_ge(max_taken, NP * (n + 1) + 2 * NP * it)
                    late = max_diag[n % 2][:, :, TPB // 2:TPB]
                    dve.tensor_tensor(late, late, max_full[n % 2][:], ALU.max).then_inc(max_joined, 1)
                if s == (GROUPS - 1) * NU:
                    invert(0)
                v, n = (s + AHEAD) % NU, (s + AHEAD) // NU + 1
                if not 0 <= n < GROUPS:
                    return
                for m in PLAN[v]:
                    j, i, _, keys, diagonal = PIECES[m]
                    wait_apart(dve, max_scored, NP * n + m + 1 + 2 * NP * it)
                    scores = ps[:, MAX_BANK + m % MAX_RING, 0:keys]
                    if diagonal:
                        dve.tensor_tensor_reduce(max_junk[:, m % MAX_RING, 0:keys], scores, mask[:, BANK - keys:BANK], 1.0,
                                                 -3e38, ALU.add, ALU.max,
                                                 max_diag[n % 2][:, j, i:i + 1]).then_inc(max_taken, 1)
                    else:
                        i -= TPB // 2
                        dve.tensor_reduce(max_full[n % 2][:, j, i:i + 1], scores, AX.X,
                                          ALU.max).then_inc(max_taken, 1)

            def invert(b):
                dve.wait_ge(sums_loaded, 16 * (b + 1))
                dve.reciprocal(inv[:, b, :], sums[:, b, :]).then_inc(inverted, 1)

            run_units(dve, unit_step)
            invert(1)

            def output_step(s, it):
                t = s + 2
                if 0 <= t < TILES:
                    dve.wait_ge(proj_done, t + 1 + 4 * it)
                    dve.wait_ge(xr_loaded[t % 4], 16 * (t // 4 + 1) + 16 * it)
                    dve.tensor_tensor(x2[t % 4][:], ps[:, O_BANK[t % 2], :], x2[t % 4][:],
                                      ALU.add).then_inc(x2_ready, 1)
                    dve.wait_ge(x2_ready, t + 1 + 4 * it)
                    dve.bn_stats(y_stat[:], x2[t % 4][:]).then_inc(y_stats, 1)
                    wait_apart(dve, y_stats, t + 1 + 4 * it)
                    dve.bn_aggr(y_mv[t % 2][:], y_stat[:]).then_inc(y_var, 1)
                if 0 <= t < TILES:
                    dve.wait_ge(y_dev, t + 1 + 4 * it)
                    dve.reciprocal(y_rs[t % 2][:], y_sd[t % 2][:]).then_inc(y_inv, 1)
                    dve.wait_ge(y_inv, t + 1 + 4 * it)
                    if t >= 2:
                        dve.wait_ge(yt_done, t - 1 + 4 * it)
                    dve.tensor_scalar(yn[t % 2][:], x2[t % 4][:], y_mv[t % 2][:, 0:1], y_rs[t % 2][:],
                                      ALU.subtract, ALU.mult).then_inc(y_normed, 1)
                t = s + 1
                if 0 <= t < TILES:
                    dve.wait_ge(yt_hi_ready, t + 1 + 4 * it)
                    dve.tensor_tensor(yt_lo[t % 2][:].rearrange("p c t -> p (c t)"), ps[:, YT_BANK[t % 2], :],
                                      yt_hi[t % 2][:].bitcast(F32).rearrange("p c t -> p (c t)"),
                                      ALU.subtract).then_inc(yt_ready, 1)
                t = s
                if 0 <= t < TILES:
                    dve.wait_ge(ff_done, t + 1 + 4 * it)
                    if t >= 2:
                        dve.wait_ge(y_stored[t % 2], 16 * (t // 2) + 32 * it)
                    dve.tensor_tensor(y_out[t % 2][:], ps[:, FF_BANK[t % 2], :], x2[t % 4][:],
                                      ALU.add).then_inc(y_ready, 1)

            run_outputs(dve, output_step)

        @block.tensor
        def _(pe):
            def product(to, hi, lo, w_hi, w_lo):
                for c in range(DC):
                    pe.matmul(to, hi[:, c, :], w_hi[:, c, :], start=(c == 0), stop=False)
                    pe.matmul(to, hi[:, c, :], w_lo[:, c, :], start=False, stop=False)
                    last = pe.matmul(to, lo[:, c, :], w_hi[:, c, :], start=False, stop=(c == DC - 1))
                return last

            def turn(bank, rows):
                for c in range(DC):
                    last = pe.transpose(ps[:, bank, c * P:(c + 1) * P], rows[:, c * P:(c + 1) * P], ident[:])
                return last

            pe.wait_ge(ident_ready, 2)

            def tile_step(s, it):
                t = s + 1
                if 0 <= t < TILES:
                    pe.wait_ge(x_normed, t + 1 + 2 * it)
                    if t >= 1:
                        pe.wait_ge(xt_ready, t + 2 * it)
                    turn(XT_BANK, xn[t % 2]).then_inc(xt_done, 1)
                t = s
                if 0 <= t < TILES:
                    if t == 0:
                        pe.wait_ge(wqkv_ready, DC)
                    pe.wait_ge(xt_ready, t + 1 + 2 * it)
                    if t >= 2:
                        pe.wait_ge(qk_clipped, t - 1 + 2 * it)
                    for i in range(2):
                        last = product(ps[:, QK_BANK[t % 2] + i, :], xt_hi[t % 2], xt_lo[t % 2],
                                       wqkv_hi[:, :, i * D:(i + 1) * D], wqkv_lo[:, :, i * D:(i + 1) * D])
                    last.then_inc(qk_done, 1)
                    if t >= 1:
                        pe.wait_ge(v_clipped, t + 2 * it)
                    product(ps[:, V_BANK, :], xt_hi[t % 2], xt_lo[t % 2],
                            wqkv_hi[:, :, 2 * D:3 * D], wqkv_lo[:, :, 2 * D:3 * D]).then_inc(v_done, 1)
                t = s - 1
                if 0 <= t < TILES:
                    pe.wait_ge(qk_ready, t + 1 + 2 * it)
                    if t >= 1:
                        pe.wait_ge(rest_ready, t + 2 * it)
                    turn(QKT_BANK, qk[t % 2][:, 0, :])
                    turn(QKT_BANK + 1, qk[t % 2][:, 1, :]).then_inc(qkt_done, 1)

            run_tiles(pe, tile_step, -1, TILES)
            pe.wait_ge(mask_ready, 2)
            pe.wait_ge(rest_ready, TILES)
            pe.wait_ge(v_clipped, TILES)

            def unit_step(s, it):
                v, n_max = (s + AHEAD) % NU, (s + AHEAD) // NU + 1
                pieces = list(PLAN[v]) if 0 <= n_max < GROUPS else []
                n = n_max - 1
                turned = v == 0 and 0 <= n < GROUPS
                if turned:
                    pe.wait_ge(max_joined, n + 1 + 2 * it)
                    pe.transpose(ps[0:G * TPB, MAX_BANK, 0:P],
                                 max_diag[n % 2][:].rearrange("p j i -> p (j i)"), ident[:]).then_inc(max_turned, 1)

                def max_piece():
                    if not pieces:
                        return
                    m = pieces.pop(0)
                    j, i, key, keys, _ = PIECES[m]
                    if m == 0:
                        pe.wait_ge(max_loaded[n_max % 2], 128 * (n_max // 2 + 1) + 128 * it)
                        if n_max >= 1:
                            pe.wait_ge(shift_hi_ready, 2 * n_max + 4 * it)
                    if NP * n_max + m >= MAX_RING:
                        pe.wait_ge(max_taken, NP * n_max + m - MAX_RING + 1 + 2 * NP * it)
                    rows = MAX_K + BIAS_ROWS
                    pe.matmul(ps[:, MAX_BANK + m % MAX_RING, 0:keys],
                              max_q[n_max % 2][0:rows, j, i * P:(i + 1) * P],
                              max_k[n_max % 2][0:rows, j, key:key + keys],
                              start=True, stop=True).then_inc(max_scored, 1)

                if 0 <= s < GROUPS * NU:
                    u, n = s % NU, s // NU
                    first_q, cols = unit_columns(u)
                    kb = UNITS[u][1]
                    rows = EXP_K + BIAS_ROWS + SHIFT_ROWS
                    if u == 0:
                        pe.wait_ge(exp_loaded[n % 2], 224 * (n // 2 + 1) + 224 * it)
                        pe.wait_ge(shift_loaded[n % 2], 32 * (n // 2 + 1) + 32 * it)
                    for pair in range(2):
                        if s >= 1:
                            pe.wait_ge(exp_done, 2 * s - 1 + pair + 4 * NU * it)
                        for j in range(2):
                            last = pe.matmul(ps[:, EXP_BANK[pair] + j, 0:cols],
                                             exp_k[n % 2][0:rows, 2 * pair + j, kb * P:(kb + 1) * P],
                                             exp_q[n % 2][0:rows, 2 * pair + j, first_q:first_q + cols],
                                             start=True, stop=not is_diagonal(u))
                            if is_diagonal(u):
                                last = pe.matmul(ps[:, EXP_BANK[pair] + j, 0:P], ident_half[:], mask_turned[:],
                                                 start=False, stop=True)
                        last.then_inc(scored, 1)
                        if not turned or pair:
                            max_piece()
                w = s - LAG
                if 0 <= w < GROUPS * NU:
                    u, n = w % NU, w // NU
                    half, kb = UNITS[u]
                    first_q, cols = unit_columns(u)
                    if u == 0:
                        pe.wait_ge(v_loaded[n % 2], 16 * (n // 2 + 1) + 16 * it)
                    if kb == 0 and 2 * n + half >= 1:
                        pe.wait_ge(o_ready, 2 * n + half + 4 * it)
                    pe.wait_ge(exp_done, 2 * (w + 1) + 4 * NU * it)
                    to = first_q - half * BANK
                    last_kb = (half + 1) * TPB // 2 - 1
                    for j in range(G):
                        last = pe.matmul(ps[j * VW:(j + 1) * VW, PV_BANK, to:to + cols],
                                         v_sb[n % 2][:, kb, j * VW:(j + 1) * VW],
                                         probs[w % P_SLOTS][:, j, 0:cols],
                                         start=(kb == 0), stop=(kb == last_kb))
                    last.then_inc(pv_done, 1)
                while pieces:
                    max_piece()

            run_units(pe, unit_step)
            pe.wait_ge(o_ready, 2 * GROUPS)

            def output_step(s, it):
                t = s + 2
                if 0 <= t < TILES:
                    if t == 0:
                        pe.wait_ge(wout_ready, DC)
                    pe.wait_ge(att_lo_ready, t + 1 + 4 * it)
                    if t >= 2:
                        pe.wait_ge(x2_ready, t - 1 + 4 * it)
                    product(ps[:, O_BANK[t % 2], :], att_hi[t % 2], att_lo[t % 2],
                            wout_hi, wout_lo).then_inc(proj_done, 1)
                t = s + 1
                if 0 <= t < TILES:
                    pe.wait_ge(y_normed, t + 1 + 4 * it)
                    if t >= 2:
                        pe.wait_ge(yt_ready, t - 1 + 4 * it)
                    turn(YT_BANK[t % 2], yn[t % 2]).then_inc(yt_done, 1)
                t = s
                if 0 <= t < TILES:
                    if t == 0:
                        pe.wait_ge(wffn_ready, DC)
                    pe.wait_ge(yt_ready, t + 1 + 4 * it)
                    if t >= 2:
                        pe.wait_ge(y_ready, t - 1 + 4 * it)
                    product(ps[:, FF_BANK[t % 2], :], yt_hi[t % 2], yt_lo[t % 2],
                            wffn_hi, wffn_lo).then_inc(ff_done, 1)

            run_outputs(pe, output_step)


def alibi_rows(bf16):
    steps = np.arange(1, HEADS + 1, dtype=np.float32) * (ALIBI_MAX / HEADS)
    slopes = (1.0 / np.power(2.0, steps)).astype(np.float32)
    bias = slopes[:, None].astype(np.float64) * np.arange(SEQ) / SCALE
    rows = np.ones((2, BIAS_ROWS + SHIFT_ROWS, HEADS, SEQ), dtype=bf16)
    for n in range(3):
        part = bias.astype(np.float32).astype(bf16)
        bias = bias - part.astype(np.float64)
        rows[1, 2 * n] = part
        rows[0, 2 * n + 1] = -part
    return rows


def kernel(L0_attn_hidden_states, L0_attn_Wqkv, L0_attn_q_ln_w, L0_attn_q_ln_b, L0_attn_k_ln_w,
           L0_attn_k_ln_b, L0_attn_Wout, L0_ffn_bases, L0_ffn_alphas):
    import ml_dtypes
    import concourse.bacc as bacc
    from concourse.bass_utils import run_bass_kernel_spmd

    x = np.asarray(L0_attn_hidden_states)
    arrays = {
        "x": np.ascontiguousarray(x.reshape(TILES, P, D)),
        "wqkv_t": np.ascontiguousarray(np.asarray(L0_attn_Wqkv).T),
        "qk_w": np.stack([np.asarray(L0_attn_q_ln_w), np.asarray(L0_attn_k_ln_w)]),
        "qk_b": np.stack([np.asarray(L0_attn_q_ln_b), np.asarray(L0_attn_k_ln_b)]),
        "wout_t": np.ascontiguousarray(np.asarray(L0_attn_Wout).T),
        "bases_t": np.ascontiguousarray(np.asarray(L0_ffn_bases).transpose(0, 2, 1)),
        "alphas": np.ascontiguousarray(np.asarray(L0_ffn_alphas)[:, :, 0]),
        "bias_rows": alibi_rows(ml_dtypes.bfloat16),
    }
    nc = bacc.Bacc("TRN2", target_bir_lowering=False, num_devices=1)
    args = [nc.dram_tensor(f"in_{k}", a.shape, mybir.dt.from_np(a.dtype), kind="ExternalInput").ap()
            for k, a in arrays.items()]
    out = nc.dram_tensor("out", (TILES, P, D), F32, kind="ExternalOutput").ap()
    build(nc, *args, out)
    r = run_bass_kernel_spmd(nc, [{f"in_{k}": a for k, a in arrays.items()}], core_ids=[0])
    return r.results[0]["out"].reshape(x.shape)
```

```python
from contextlib import ExitStack

import numpy as np

import concourse.bass as bass
from concourse import mybir

F32 = mybir.dt.float32
F32R = mybir.dt.float32r
BF16 = mybir.dt.bfloat16
ALU = mybir.AluOpType
ACT = mybir.ActivationFunctionType
AX = mybir.AxisListType
ds = bass.ds

P = 128
BANK = 512
D = 512
DC = D // P
BATCH, SEQ = 2, 1024
TILES = BATCH * SEQ // P
TPB = SEQ // P
HEADS, HD = 32, 16
G = 4
GROUPS = BATCH * HEADS // G
GPB = HEADS // G
VW = 32
CLIP = 8.0
EPS = 1e-5
SCALE = HD ** -0.5
ALIBI_MAX = 8.0
MASKED = -1e30

TERMS = [(0, 0), (0, 1), (1, 0), (1, 1), (0, 2), (2, 0)]
MAX_TERMS = 3
BIAS_ROWS = 6
SHIFT_ROWS = 2
EXP_K = len(TERMS) * HD
MAX_K = MAX_TERMS * HD

UNITS = [(h, kb) for h in range(2) for kb in range((h + 1) * TPB // 2)]
NU = len(UNITS)
LAG = 2
AHEAD = 4
P_SLOTS = 3
MAX_RING = 3
TURN_SLOT = 2


def unit_columns(u):
    half, kb = UNITS[u]
    first = max(kb * P, half * BANK)
    return first, (half + 1) * BANK - first


def is_diagonal(u):
    half, kb = UNITS[u]
    return kb * P >= half * BANK




def max_pieces():
    out = []
    for j in range(G):
        for i in range(TPB):
            keys = (i + 1) * P
            if keys > BANK:
                out.append((j, i, 0, BANK, False))
                out.append((j, i, BANK, keys - BANK, True))
            else:
                out.append((j, i, 0, keys, True))
    return out


PIECES = max_pieces()
NP = len(PIECES)
assert NP % MAX_RING == 0 and (2 * NU) % P_SLOTS == 0


SLOTS = 3


def piece_plan():
    slots = []
    for v in range(NU):
        u, w = (v + NU - AHEAD) % NU, (v + 2 * NU - AHEAD - LAG) % NU
        qk_cols = 2 * (unit_columns(u)[1] + (P if is_diagonal(u) else 0))
        slots += [qk_cols, 4 * unit_columns(w)[1], qk_cols]
    total, pe_all, at = sum(n for _, _, _, n, _ in PIECES), sum(slots), 0
    plan, pe_time, done = [], 0, 0
    for k, cols in enumerate(slots):
        pe_time += cols
        mine = []
        while at < NP and (at == k if k < 2 else done + PIECES[at][3] / 2 <= pe_time * total / pe_all
                           or k == len(slots) - 1):
            mine.append(at)
            done += PIECES[at][3]
            at += 1
            if k < 2:
                break
        plan.append(mine)
    return [plan[SLOTS * v:SLOTS * (v + 1)] for v in range(NU)]


PLAN = piece_plan()

STACKS_AT = 12
assert STACKS_AT - 2 >= TPB
WEIGHTS_AT = [2, 4, 6, 8, 9, 10, NU + LAG - 1, NU + LAG]


def build(nc, x, wqkv_t, qk_w, qk_b, wout_t, bases_t, alphas, bias_rows, out):
    ctx = ExitStack()

    def alloc(stack):
        def sb(name, shape, dt=F32):
            return stack.enter_context(nc.sbuf_tensor(name, shape, dt))
        return sb

    def sem(name):
        return ctx.enter_context(nc.semaphore(name))

    parts_dram = nc.dram_tensor("parts_dram", [2, 3, BATCH, D, SEQ], BF16).ap()
    v_dram = nc.dram_tensor("v_dram", [BATCH, GPB, TPB, P, G * VW], F32).ap()
    o_dram = nc.dram_tensor("o_dram", [BATCH, VW, HEADS, SEQ], F32).ap()
    inv_dram = nc.dram_tensor("inv_dram", [BATCH, HEADS, SEQ], F32).ap()

    with ctx:
        sb = alloc(ctx)
        ident = sb("ident", [P, P])
        ident_half = sb("ident_half", [P, P], BF16)
        mask = sb("mask", [P, BANK], BF16)
        mask_turned = sb("mask_turned", [P, P], BF16)
        eps = sb("eps", [P, 1])
        wout_hi = sb("wout_hi", [P, DC, D], F32R)
        wout_lo = sb("wout_lo", [P, DC, D], F32R)
        wffn_hi = sb("wffn_hi", [P, DC, D], F32R)
        wffn_lo = sb("wffn_lo", [P, DC, D], F32R)
        wffn_term = sb("wffn_term", [P, 2, D])

        with ExitStack() as staging:
            wqkv_raw = alloc(staging)("wqkv_raw", [P, DC, 3 * D])
        sb = alloc(ctx)
        max_q = [sb(f"max_q{i}", [P, G, SEQ], BF16) for i in range(2)]
        max_k = [sb(f"max_k{i}", [P, G, SEQ], BF16) for i in range(2)]
        exp_q = [sb(f"exp_q{i}", [P, G, SEQ], BF16) for i in range(2)]
        exp_k = [sb(f"exp_k{i}", [P, G, SEQ], BF16) for i in range(2)]

        with ExitStack() as first:
            sb = alloc(first)
            wqkv_hi = sb("wqkv_hi", [P, DC, 3 * D], F32R)
            wqkv_lo = sb("wqkv_lo", [P, DC, 3 * D], F32R)
            qk_gain = sb("qk_gain", [P, 2, D])
            qk_bias = sb("qk_bias", [P, 2, D])
            x_in = [sb(f"x_in{i}", [P, D]) for i in range(2)]
            xn = [sb(f"xn{i}", [P, D]) for i in range(2)]
            xt_hi = [sb(f"xt_hi{i}", [P, DC, P], F32R) for i in range(2)]
            xt_lo = [sb(f"xt_lo{i}", [P, DC, P], F32R) for i in range(2)]
            qk = [sb(f"qk{i}", [P, 2, D]) for i in range(2)]
            v_ext = [sb(f"v_ext{i}", [P, HEADS, VW]) for i in range(2)]
            rest = sb("rest", [P, 2, DC, P])
            parts = sb("parts", [P, 3, 2, DC, 2 * P], BF16)
            x_stat = sb("x_stat", [P, 6])
            x_mv = [sb(f"x_mv{i}", [P, 2]) for i in range(2)]
            x_sd = [sb(f"x_sd{i}", [P, 1]) for i in range(2)]
            x_rs = [sb(f"x_rs{i}", [P, 1]) for i in range(2)]
            qk_stat = sb("qk_stat", [P, 2, 6])
            qk_mv = [sb(f"qk_mv{i}", [P, 2, 2]) for i in range(2)]
            qk_sd = [sb(f"qk_sd{i}", [P, 2]) for i in range(2)]
            qk_rs = [sb(f"qk_rs{i}", [P, 2]) for i in range(2)]
        sb = alloc(ctx)
        probs = [sb(f"probs{i}", [P, G, BANK]) for i in range(P_SLOTS)]
        v_sb = [sb(f"v_sb{i}", [P, TPB, G * VW]) for i in range(2)]
        o_sb = [sb(f"o_sb{i}", [P, BANK]) for i in range(2)]
        max_junk = sb("max_junk", [P, MAX_RING, BANK], BF16)
        max_diag = [sb(f"max_diag{i}", [P, G, TPB]) for i in range(2)]
        max_full = [sb(f"max_full{i}", [P, G, TPB // 2]) for i in range(2)]
        shift = [sb(f"shift{i}", [G * TPB, P]) for i in range(2)]
        shift_hi = [sb(f"shift_hi{i}", [G * TPB, P], BF16) for i in range(2)]
        shift_mid = [sb(f"shift_mid{i}", [G * TPB, P], BF16) for i in range(2)]
        with ExitStack() as staging:
            sb = alloc(staging)
            wout_raw = sb("wout_raw", [P, DC, D])
            bases_sb = sb("bases_sb", [P, 4, DC, D], BF16)
            alpha_sb = sb("alpha_sb", [P, 4, D])
            wffn_sum = sb("wffn_sum", [P, DC, D])
        sb = alloc(ctx)
        o_in = [sb(f"o_in{i}", [P, DC, P]) for i in range(2)]
        inv_in = [sb(f"inv_in{i}", [P, P]) for i in range(2)]
        sums = sb("sums", [P, BATCH, HEADS * SEQ // P])
        inv = sb("inv", [P, BATCH, HEADS * SEQ // P])
        att = [sb(f"att{i}", [P, DC, P]) for i in range(2)]
        att_hi = [sb(f"att_hi{i}", [P, DC, P], F32R) for i in range(2)]
        att_lo = [sb(f"att_lo{i}", [P, DC, P], F32R) for i in range(2)]
        x2 = [sb(f"x2_{i}", [P, D]) for i in range(4)]
        yn = [sb(f"yn{i}", [P, D]) for i in range(2)]
        yt_hi = [sb(f"yt_hi{i}", [P, DC, P], F32R) for i in range(2)]
        yt_lo = [sb(f"yt_lo{i}", [P, DC, P], F32R) for i in range(2)]
        y_out = [sb(f"y_out{i}", [P, D]) for i in range(2)]
        y_stat = sb("y_stat", [P, 6])
        y_mv = [sb(f"y_mv{i}", [P, 2]) for i in range(2)]
        y_sd = [sb(f"y_sd{i}", [P, 1]) for i in range(2)]
        y_rs = [sb(f"y_rs{i}", [P, 1]) for i in range(2)]

        ps = ctx.enter_context(nc.psum_tensor("ps", [P, 8, BANK], F32))
        XT_BANK, QK_BANK, V_BANK, QKT_BANK = 0, (1, 3), 5, 6
        EXP_BANK, PV_BANK, MAX_BANK = (0, 2), 4, 5
        O_BANK, YT_BANK, FF_BANK = (0, 1), (2, 3), (4, 5)

        ident_zero, ident_ready, mask_zero, mask_ready = (
            sem("ident_zero"), sem("ident_ready"), sem("mask_zero"), sem("mask_ready"))
        eps_ready, ones_ready = sem("eps_ready"), sem("ones_ready")
        wqkv_loaded = [sem(f"wqkv_loaded{c}") for c in range(DC)]
        gain_loaded, wout_loaded, bases_loaded, alphas_loaded = (
            sem("gain_loaded"), sem("wout_loaded"), sem("bases_loaded"), sem("alphas_loaded"))
        wqkv_hi_ready, wqkv_ready = sem("wqkv_hi_ready"), sem("wqkv_ready")
        wout_hi_ready, wout_ready = sem("wout_hi_ready"), sem("wout_ready")
        wffn_term_ready, wffn_summed = sem("wffn_term_ready"), sem("wffn_summed")
        wffn_hi_ready, wffn_ready = sem("wffn_hi_ready"), sem("wffn_ready")
        waits_passed = [sem("waits_passed_dve"), sem("waits_passed_pool")]
        x_loaded = [sem(f"x_loaded{i}") for i in range(2)]
        x_stats, x_var, x_dev, x_inv, x_normed = (
            sem("x_stats"), sem("x_var"), sem("x_dev"), sem("x_inv"), sem("x_normed"))
        xt_done, xt_hi_ready, xt_ready = sem("xt_done"), sem("xt_hi_ready"), sem("xt_ready")
        qk_done, v_done = sem("qk_done"), sem("v_done")
        qk_clipped, v_clipped = sem("qk_clipped"), sem("v_clipped")
        qk_stats, qk_var, qk_dev, qk_inv, qk_normed = (
            sem("qk_stats"), sem("qk_var"), sem("qk_dev"), sem("qk_inv"), sem("qk_normed"))
        qk_scaled, qk_ready = sem("qk_scaled"), sem("qk_ready")
        qkt_done, hi_ready, rest_ready, mid_ready, lo_ready = (
            sem("qkt_done"), sem("hi_ready"), sem("rest_ready"), sem("mid_ready"), sem("lo_ready"))
        v_stored = [sem(f"v_stored{i}") for i in range(2)]
        parts_stored = sem("parts_stored")
        max_loaded = [sem(f"max_loaded{i}") for i in range(2)]
        exp_loaded = [sem(f"exp_loaded{i}") for i in range(2)]
        v_loaded = [sem(f"v_loaded{i}") for i in range(2)]
        shift_loaded = [sem(f"shift_loaded{i}") for i in range(2)]
        max_scored, max_taken, max_joined, max_turned = (
            sem("max_scored"), sem("max_taken"), sem("max_joined"), sem("max_turned"))
        shift_hi_ready, shift_ready = sem("shift_hi_ready"), sem("shift_ready")
        scored, exp_done, pv_done, o_ready = (
            sem("scored"), sem("exp_done"), sem("pv_done"), sem("o_ready"))
        o_stored = [sem(f"o_stored{i}") for i in range(2)]
        o_loaded = [sem(f"o_loaded{i}") for i in range(2)]
        xr_loaded = [sem(f"xr_loaded{i}") for i in range(4)]
        sums_loaded, inverted, inv_stored = sem("sums_loaded"), sem("inverted"), sem("inv_stored")
        att_ready, att_hi_ready, att_lo_ready = (
            sem("att_ready"), sem("att_hi_ready"), sem("att_lo_ready"))
        proj_done, x2_ready = sem("proj_done"), sem("x2_ready")
        y_stats, y_var, y_dev, y_inv, y_normed = (
            sem("y_stats"), sem("y_var"), sem("y_dev"), sem("y_inv"), sem("y_normed"))
        yt_done, yt_hi_ready, yt_ready = sem("yt_done"), sem("yt_hi_ready"), sem("yt_ready")
        ff_done, y_ready = sem("ff_done"), sem("y_ready")
        y_stored = [sem(f"y_stored{i}") for i in range(2)]

        block = ctx.enter_context(nc.Block())

        def run(eng, step, first, last, body, loop_first, rounds):
            for s in range(first, loop_first):
                step(s, 0)
            with eng.Fori(0, rounds) as it:
                for s in range(loop_first, loop_first + body):
                    step(s, it)
            for s in range(loop_first + body * rounds, last + 1):
                step(s, 0)

        def wait_apart(eng, semaphore, value):
            eng.wait_ge(semaphore, value)
            eng.sem_inc(waits_passed[eng is nc.gpsimd], 1)

        def run_tiles(eng, step, first, last):
            run(eng, step, first, last, 2, 4, 4)

        def run_units(eng, step):
            run(eng, step, -NU - AHEAD, GROUPS * NU + LAG - 1, 2 * NU, NU + LAG + 1, GROUPS // 2 - 2)

        def run_groups(eng, step):
            run(eng, step, -2, GROUPS, 2, 1, GROUPS // 2 - 2)

        def run_outputs(eng, step):
            run(eng, step, -4, TILES - 1, 4, 2, 2)

        @block.sync
        def _(sp):
            sp.dma_start(x_in[0][:], x[0]).then_inc(x_loaded[0], 16)
            for c in range(DC):
                sp.dma_start(wqkv_raw[:, c, :], wqkv_t[c * P:(c + 1) * P, :]).then_inc(wqkv_loaded[c], 16)
            sp.dma_start(x_in[1][:], x[1]).then_inc(x_loaded[1], 16)
            for i in range(2):
                sp.dma_start(qk_gain[:, i, :], qk_w[i:i + 1, :].partition_broadcast(P)).then_inc(gain_loaded, 16)
                sp.dma_start(qk_bias[:, i, :], qk_b[i:i + 1, :].partition_broadcast(P)).then_inc(gain_loaded, 16)

            def tile_step(s, it):
                t = s + 3
                if 2 <= t < TILES:
                    sp.wait_ge(x_normed, t - 1 + 2 * it)
                    sp.dma_start(x_in[t % 2][:], x[t + 2 * it]).then_inc(x_loaded[t % 2], 16)
                t = s
                if 0 <= t < TILES:
                    sp.wait_ge(v_clipped, t + 1 + 2 * it)
                    tt = t + 2 * it
                    sp.dma_start(v_dram[tt // TPB, :, tt % TPB, :, :].rearrange("g p n -> p g n"),
                                 v_ext[t % 2][:].rearrange("p (g h) n -> p g (h n)", g=GPB)
                                 ).then_inc(v_stored[t % 2], 16)
                t = s - 2
                if 0 <= t < TILES and t % 2:
                    sp.wait_ge(lo_ready, t + 1 + 2 * it)
                    sp.wait_ge(mid_ready, t + 1 + 2 * it)
                    tt = t - 1 + 2 * it
                    for n in range(3):
                        for i in range(2):
                            sp.dma_start(
                                parts_dram[i, n, tt // TPB, :, ds((tt % TPB) * P, 2 * P)]
                                .rearrange("(c p) t -> p c t", p=P),
                                parts[:, n, i, :, :]).then_inc(parts_stored, 16)

            def projections_over():
                sp.wait_ge(parts_stored, 6 * 16 * TILES // 2)
                for i in range(2):
                    sp.wait_ge(v_stored[i], 16 * TILES // 2)
                sp.wait_ge(qkt_done, TILES)
                sp.wait_ge(lo_ready, TILES)

            def load_last_weights():
                for k in range(4):
                    sp.dma_start(alpha_sb[:, k, :], alphas[k:k + 1, :].partition_broadcast(P)).then_inc(alphas_loaded, 16)
                sp.dma_start(wout_raw[:], wout_t.rearrange("(c p) o -> p c o", p=P)).then_inc(wout_loaded, 16)

            def stack(dst_q, dst_k, terms, n, it, loaded):
                nn = n + 2 * it
                for i, dst in ((0, dst_q), (1, dst_k)):
                    for r, term in enumerate(terms):
                        src = parts_dram[i, term[i]].rearrange("b f t -> (b f) t")
                        sp.dma_start(dst[r * HD:(r + 1) * HD, :, :],
                                     src[ds(nn * (G * HD), G * HD), :].rearrange("(j d) t -> d j t", j=G)
                                     ).then_inc(loaded, 16)
                    r = len(terms) * HD
                    rows = BIAS_ROWS + (SHIFT_ROWS if i == 1 and len(terms) > MAX_TERMS else 0)
                    sp.dma_start(dst[r:r + rows, :, :],
                                 bias_rows[i, 0:rows, ds((nn % GPB) * G, G), :]).then_inc(loaded, 16)

            def tile_step_and_stacks(s, it):
                tile_step(s, it)
                if s == STACKS_AT:
                    sp.wait_ge(parts_stored, 6 * 16 * (STACKS_AT - 2) // 2)
                    sp.wait_ge(wqkv_ready, DC)
                    for n in range(2):
                        load_max(n, 0)
                    load_exp(0, 0)

            def load_max(n, it):
                stack(max_q[n % 2], max_k[n % 2], TERMS[:MAX_TERMS], n, it, max_loaded[n % 2])

            def load_exp(n, it):
                stack(exp_q[n % 2], exp_k[n % 2], TERMS, n, it, exp_loaded[n % 2])

            run_tiles(sp, tile_step_and_stacks, -1, TILES + 1)
            projections_over()

            def group_step(s, it):
                n = s + 2
                if 2 <= n < GROUPS:
                    sp.wait_ge(max_scored, NP * (n - 1) + 2 * NP * it)
                    load_max(n, it)
                n = s + 1
                if 0 <= n < GROUPS:
                    if n >= 2:
                        sp.wait_ge(scored, 2 * NU * (n - 1) + 4 * NU * it)
                    if n >= 1:
                        load_exp(n, it)
                    if n >= 2:
                        sp.wait_ge(pv_done, NU * (n - 1) + 2 * NU * it)
                    nn = n + 2 * it
                    sp.dma_start(v_sb[n % 2][:], v_dram.rearrange("b g k p n -> (b g) k p n")[nn]
                                 .rearrange("k p n -> p k n")).then_inc(v_loaded[n % 2], 16)
                if s == 0:
                    load_last_weights()
                for n, half in ((s - 1, 1), (s, 0)):
                    if 0 <= n < GROUPS:
                        sp.wait_ge(o_ready, 2 * n + half + 1 + 4 * it)
                        nn = n + 2 * it
                        sp.dma_start(o_dram[nn // GPB, :, ds((nn % GPB) * G, G), half * BANK:(half + 1) * BANK]
                                     .rearrange("r j t -> j r t"), o_sb[half][:]).then_inc(o_stored[half], 16)
                n = s + 1
                if 0 <= n < GROUPS:
                    sp.wait_ge(shift_ready, n + 1 + 2 * it)
                    for r, part in ((0, shift_hi), (1, shift_mid)):
                        row = EXP_K + BIAS_ROWS + r
                        sp.dma_start(exp_q[n % 2][row:row + 1, :, :].rearrange("p j t -> p (j t)"),
                                     part[n % 2][:]).then_inc(shift_loaded[n % 2], 16)

                if s == GROUPS - 2:
                    load_sums(0)
                if s == GROUPS - 1:
                    store_inverses(0)
                    sp.wait_ge(inv_stored, 16)
                    sp.wait_ge(wout_ready, DC)
                    sp.wait_ge(wffn_ready, DC)
                    for t in range(2):
                        load_sums_of_tile(t, 0)
                        load_residual(t, 0)

            def load_sums_of_tile(t, it):
                tt = t + 4 * it
                sp.dma_start(o_in[t % 2][:], o_dram[tt // TPB, 0:HD, :, ds((tt % TPB) * P, P)]
                             .rearrange("(c r) h t -> (r h) c t", c=DC)).then_inc(o_loaded[t % 2], 16)
                rows = inv_dram[tt // TPB, :, ds((tt % TPB) * P, P)]
                sp.dma_start(inv_in[t % 2][:], rows.rearrange("(a h) t -> a h t", a=1)
                             .broadcast_to([HD // DC, HEADS, P])).then_inc(o_loaded[t % 2], 16)

            def load_residual(t, it):
                sp.dma_start(x2[t % 4][:], x[t + 4 * it]).then_inc(xr_loaded[t % 4], 16)

            def load_sums(b):
                for half in range(2):
                    sp.wait_ge(o_stored[half], 16 * (GROUPS if b else GROUPS - 1 - half))
                sp.dma_start(sums[:, b, :], o_dram[b, HD].rearrange("h (q t) -> (h q) t", q=P // HEADS)
                             ).then_inc(sums_loaded, 16)

            def store_inverses(b):
                sp.wait_ge(inverted, b + 1)
                sp.dma_start(inv_dram[b].rearrange("h (q t) -> (h q) t", q=P // HEADS),
                             inv[:, b, :]).then_inc(inv_stored, 16)

            run_groups(sp, group_step)
            load_sums(1)

            def output_step(s, it):
                t = s + 4
                if 2 <= t < TILES:
                    sp.wait_ge(att_ready, t - 1 + 4 * it)
                    load_sums_of_tile(t, it)
                t = s + 3
                if 2 <= t < TILES:
                    if t >= 4:
                        sp.wait_ge(y_ready, t - 3 + 4 * it)
                    load_residual(t, it)
                t = s
                if 0 <= t < TILES:
                    sp.wait_ge(y_ready, t + 1 + 4 * it)
                    sp.dma_start(out[t + 4 * it], y_out[t % 2][:]).then_inc(y_stored[t % 2], 16)
                if s == 0:
                    store_inverses(1)
                if s == 1:
                    sp.wait_ge(inv_stored, 16 * BATCH)

            run_outputs(sp, output_step)
            for i in range(2):
                sp.wait_ge(y_stored[i], 16 * TILES // 2)

        @block.gpsimd
        def _(pool):
            pool.memset(eps[:], EPS).then_inc(eps_ready, 1)
            pool.memset(ident[:], 0.0).then_inc(ident_zero, 1)
            pool.wait_ge(ident_zero, 1)
            pool.affine_select(out=ident[:], in_=ident[:], compare_op=ALU.not_equal, fill=1.0, base=0,
                               pattern=[[-1, P]], channel_multiplier=1).then_inc(ident_ready, 1)
            pool.memset(ident_half[:], 0.0).then_inc(ident_zero, 1)
            pool.wait_ge(ident_zero, 2)
            pool.affine_select(out=ident_half[:], in_=ident_half[:], compare_op=ALU.not_equal, fill=1.0, base=0,
                               pattern=[[-1, P]], channel_multiplier=1).then_inc(ident_ready, 1)
            pool.memset(mask_turned[:], 0.0).then_inc(mask_zero, 1)
            pool.wait_ge(mask_zero, 1)
            pool.affine_select(out=mask_turned[:], in_=mask_turned[:], compare_op=ALU.is_ge, fill=MASKED, base=0,
                               pattern=[[1, P]], channel_multiplier=-1).then_inc(mask_ready, 1)
            pool.memset(mask[:], 0.0).then_inc(mask_zero, 1)
            pool.wait_ge(mask_zero, 2)
            pool.affine_select(out=mask[:], in_=mask[:], compare_op=ALU.is_ge, fill=MASKED, base=BANK - P,
                               pattern=[[-1, BANK]], channel_multiplier=1).then_inc(mask_ready, 1)
            for i in range(2):
                pool.memset(v_ext[i][:], 1.0).then_inc(ones_ready, 1)

            def low_part(lo, whole, hi, hi_ready_, ready):
                for c in range(DC):
                    pool.wait_ge(hi_ready_, c + 1)
                    pool.tensor_tensor(lo[:, c, :], whole[:, c, :], hi[:, c, :].bitcast(F32),
                                       ALU.subtract).then_inc(ready, 1)

            def tile_step(s, it):
                t = s - 2
                if 0 <= t < TILES:
                    pool.wait_ge(mid_ready, t + 1 + 2 * it)
                    half = ds((t % 2) * P, P)
                    pool.tensor_tensor(parts[:, 2, :, :, half], rest[:], parts[:, 1, :, :, half],
                                       ALU.subtract).then_inc(lo_ready, 1)
                t = s
                if 0 <= t < TILES:
                    if t == 0:
                        pool.wait_ge(gain_loaded, 4 * 16)
                    pool.wait_ge(qk_normed, t + 1 + 2 * it)
                    pool.tensor_tensor(qk[t % 2][:], qk[t % 2][:], qk_gain[:], ALU.mult).then_inc(qk_scaled, 1)
                    pool.wait_ge(qk_scaled, t + 1 + 2 * it)
                    pool.tensor_tensor(qk[t % 2][:], qk[t % 2][:], qk_bias[:], ALU.add).then_inc(qk_ready, 1)

            run_tiles(pool, tile_step, 0, TILES + 1)

            def load_bases():
                pool.wait_ge(v_loaded[0], 16)
                for k in range(4):
                    pool.dma_start(bases_sb[:, k, :, :],
                                   bases_t[k].rearrange("(c p) o -> p c o", p=P)).then_inc(bases_loaded, 16)
                pool.wait_ge(bases_loaded, 4 * 16)
                pool.wait_ge(alphas_loaded, 4 * 16)

            def sum_bases(c):
                for k in range(4):
                    to = wffn_sum[:, c, :] if k == 0 else wffn_term[:, k % 2, :]
                    done = 3 * c + max(k - 1, 0)
                    if done:
                        pool.wait_ge(wffn_summed, done)
                    pool.tensor_tensor(to, bases_sb[:, k, c, :], alpha_sb[:, k, :],
                                       ALU.mult).then_inc(wffn_term_ready, 1)
                    if k:
                        pool.wait_ge(wffn_term_ready, 4 * c + k + 1)
                        if done:
                            pool.wait_ge(wffn_summed, done)
                        pool.tensor_tensor(wffn_sum[:, c, :], wffn_sum[:, c, :], wffn_term[:, k % 2, :],
                                           ALU.add).then_inc(wffn_summed, 1)

            def unit_step(s, it):
                n = (s + AHEAD) // NU
                if (s + AHEAD) % NU == 0 and 0 <= n < GROUPS:
                    pool.wait_ge(shift_hi_ready, 2 * (n + 1) + 4 * it)
                    pool.tensor_tensor(shift_mid[n % 2][:], shift[n % 2][:], shift_hi[n % 2][:],
                                       ALU.subtract).then_inc(shift_ready, 1)
                if s == -AHEAD:
                    load_bases()
                    for c in range(DC // 2):
                        sum_bases(c)
                if s == NU - AHEAD:
                    for c in range(DC // 2, DC):
                        sum_bases(c)
                    low_part(wout_lo, wout_raw, wout_hi, wout_hi_ready, wout_ready)

            run_units(pool, unit_step)
            low_part(wffn_lo, wffn_sum, wffn_hi, wffn_hi_ready, wffn_ready)

            def output_step(s, it):
                t = s + 3
                if 0 <= t < TILES:
                    pool.wait_ge(o_loaded[t % 2], 2 * 16 * (t // 2 + 1) + 2 * 2 * 16 * it)
                    if t >= 2:
                        pool.wait_ge(att_lo_ready, t - 1 + 4 * it)
                    pool.tensor_tensor(att[t % 2][:], o_in[t % 2][:],
                                       inv_in[t % 2][:].rearrange("p (a t) -> p a t", a=1).broadcast_to([P, DC, P]),
                                       ALU.mult).then_inc(att_ready, 1)
                    pool.wait_ge(att_hi_ready, t + 1 + 4 * it)
                    pool.tensor_tensor(att_lo[t % 2][:], att[t % 2][:], att_hi[t % 2][:].bitcast(F32),
                                       ALU.subtract).then_inc(att_lo_ready, 1)

            run_outputs(pool, output_step)

        @block.scalar
        def _(act):
            for c in range(DC):
                act.wait_ge(wqkv_loaded[c], 16)
                act.activation(wqkv_hi[:, c, :], wqkv_raw[:, c, :], ACT.Copy).then_inc(wqkv_hi_ready, 1)
            act.wait_ge(eps_ready, 1)

            def tile_step(s, it):
                t = s + 1
                if 0 <= t < TILES:
                    act.wait_ge(xt_done, t + 1 + 2 * it)
                    if t >= 2:
                        act.wait_ge(v_done, t - 1 + 2 * it)
                    act.activation(xt_hi[t % 2][:].rearrange("p c t -> p (c t)"), ps[:, XT_BANK, :],
                                   ACT.Copy).then_inc(xt_hi_ready, 1)
                t = s - 2
                half = ds((t % 2) * P, P)
                if 0 <= t < TILES:
                    act.wait_ge(qkt_done, t + 1 + 2 * it)
                    if t >= 2:
                        act.wait_ge(parts_stored, 6 * 16 * (t // 2) + 6 * 16 * it)
                    act.activation(parts[:, 0, :, :, half],
                                   ps[:, QKT_BANK:QKT_BANK + 2, :].rearrange("p i (c t) -> p i c t", c=DC),
                                   ACT.Copy).then_inc(hi_ready, 1)
                t = s + 2
                if 0 <= t < TILES:
                    act.wait_ge(x_var, t + 1 + 2 * it)
                    act.activation(x_sd[t % 2][:], x_mv[t % 2][:, 1:2], ACT.Sqrt, bias=eps[:]).then_inc(x_dev, 1)
                t = s - 2
                if 0 <= t < TILES:
                    act.wait_ge(rest_ready, t + 1 + 2 * it)
                    act.activation(parts[:, 1, :, :, half], rest[:], ACT.Copy).then_inc(mid_ready, 1)
                t = s
                if 0 <= t < TILES:
                    act.wait_ge(qk_var, t + 1 + 2 * it)
                    act.activation(qk_sd[t % 2][:], qk_mv[t % 2][:, :, 1], ACT.Sqrt, bias=eps[:]).then_inc(qk_dev, 1)

            run_tiles(act, tile_step, -2, TILES + 1)

            def unit_step(s, it):
                if s in WEIGHTS_AT:
                    c = WEIGHTS_AT.index(s)
                    if c == 0:
                        act.wait_ge(wout_loaded, 16)
                    if c < DC:
                        act.activation(wout_hi[:, c, :], wout_raw[:, c, :], ACT.Copy).then_inc(wout_hi_ready, 1)
                    else:
                        c -= DC
                        act.wait_ge(wffn_summed, 3 * (c + 1))
                        act.activation(wffn_hi[:, c, :], wffn_sum[:, c, :], ACT.Copy).then_inc(wffn_hi_ready, 1)
                for pair in range(2):
                    if 0 <= s < GROUPS * NU:
                        n = unit_columns(s % NU)[1]
                        act.wait_ge(scored, 2 * s + pair + 1 + 4 * NU * it)
                        if s >= P_SLOTS and pair == 0:
                            act.wait_ge(pv_done, s - P_SLOTS + 1 + 2 * NU * it)
                        act.activation(probs[s % P_SLOTS][:, 2 * pair:2 * pair + 2, 0:n],
                                       ps[:, EXP_BANK[pair]:EXP_BANK[pair] + 2, 0:n],
                                       ACT.Exp, scale=SCALE).then_inc(exp_done, 1)
                    if pair == 1:
                        break
                    last = s - LAG
                    if last >= 0 and last % NU in (TPB // 2 - 1, NU - 1):
                        copy_half(last, it)
                    n = (s + AHEAD) // NU
                    if (s + AHEAD) % NU == 0 and 0 <= n < GROUPS:
                        act.wait_ge(max_turned, n + 1 + 2 * it)
                        turned = ps[0:G * TPB, MAX_BANK + TURN_SLOT, 0:P]
                        act.activation(shift[n % 2][:], turned, ACT.Copy, scale=-1.0).then_inc(shift_hi_ready, 1)
                        act.activation(shift_hi[n % 2][:], turned, ACT.Copy, scale=-1.0).then_inc(shift_hi_ready, 1)

            def copy_half(u, it):
                half = 0 if u % NU == TPB // 2 - 1 else 1
                n = u // NU
                act.wait_ge(pv_done, u + 1 + 2 * NU * it)
                if n >= 1:
                    act.wait_ge(o_stored[half], 16 * n + 32 * it)
                act.activation(o_sb[half][:], ps[:, PV_BANK, :], ACT.Copy).then_inc(o_ready, 1)

            run_units(act, unit_step)

            def output_step(s, it):
                t = s + 3
                if 0 <= t < TILES:
                    act.wait_ge(att_ready, t + 1 + 4 * it)
                    if t >= 2:
                        act.wait_ge(proj_done, t - 1 + 4 * it)
                    act.activation(att_hi[t % 2][:], att[t % 2][:], ACT.Copy).then_inc(att_hi_ready, 1)
                t = s + 2
                if 0 <= t < TILES:
                    act.wait_ge(y_var, t + 1 + 4 * it)
                    act.activation(y_sd[t % 2][:], y_mv[t % 2][:, 1:2], ACT.Sqrt, bias=eps[:]).then_inc(y_dev, 1)
                t = s + 1
                if 0 <= t < TILES:
                    act.wait_ge(yt_done, t + 1 + 4 * it)
                    if t >= 2:
                        act.wait_ge(ff_done, t - 1 + 4 * it)
                    act.activation(yt_hi[t % 2][:].rearrange("p c t -> p (c t)"), ps[:, YT_BANK[t % 2], :],
                                   ACT.Copy).then_inc(yt_hi_ready, 1)

            run_outputs(act, output_step)

        @block.vector
        def _(dve):
            for c in range(DC):
                dve.wait_ge(wqkv_hi_ready, c + 1)
                dve.tensor_tensor(wqkv_lo[:, c, :], wqkv_raw[:, c, :], wqkv_hi[:, c, :].bitcast(F32),
                                  ALU.subtract).then_inc(wqkv_ready, 1)

            def tile_step(s, it):
                t = s + 1
                if 0 <= t < TILES:
                    dve.wait_ge(xt_hi_ready, t + 1 + 2 * it)
                    dve.tensor_tensor(xt_lo[t % 2][:].rearrange("p c t -> p (c t)"), ps[:, XT_BANK, :],
                                      xt_hi[t % 2][:].bitcast(F32).rearrange("p c t -> p (c t)"),
                                      ALU.subtract).then_inc(xt_ready, 1)
                t = s + 2
                if 0 <= t < TILES:
                    dve.wait_ge(x_loaded[t % 2], 16 * (t // 2 + 1) + 16 * it)
                    dve.bn_stats(x_stat[:], x_in[t % 2][:]).then_inc(x_stats, 1)
                    wait_apart(dve, x_stats, t + 1 + 2 * it)
                    dve.bn_aggr(x_mv[t % 2][:], x_stat[:]).then_inc(x_var, 1)
                t = s - 2
                if 0 <= t < TILES:
                    dve.wait_ge(hi_ready, t + 1 + 2 * it)
                    if t >= 1:
                        dve.wait_ge(lo_ready, t + 2 * it)
                    dve.tensor_tensor(rest[:],
                                      ps[:, QKT_BANK:QKT_BANK + 2, :].rearrange("p i (c t) -> p i c t", c=DC),
                                      parts[:, 0, :, :, ds((t % 2) * P, P)],
                                      ALU.subtract).then_inc(rest_ready, 1)
                t = s + 2
                if 0 <= t < TILES:
                    dve.wait_ge(x_dev, t + 1 + 2 * it)
                    dve.reciprocal(x_rs[t % 2][:], x_sd[t % 2][:]).then_inc(x_inv, 1)
                    dve.wait_ge(x_inv, t + 1 + 2 * it)
                    if t >= 2:
                        dve.wait_ge(xt_done, t - 1 + 2 * it)
                    dve.tensor_scalar(xn[t % 2][:], x_in[t % 2][:], x_mv[t % 2][:, 0:1], x_rs[t % 2][:],
                                      ALU.subtract, ALU.mult).then_inc(x_normed, 1)
                t = s
                if 0 <= t < TILES:
                    dve.wait_ge(qk_done, t + 1 + 2 * it)
                    if t >= 2:
                        dve.wait_ge(qkt_done, t - 1 + 2 * it)
                    bank = QK_BANK[t % 2]
                    dve.tensor_scalar(qk[t % 2][:], ps[:, bank:bank + 2, :], CLIP, -CLIP,
                                      ALU.min, ALU.max).then_inc(qk_clipped, 1)
                    dve.wait_ge(qk_clipped, t + 1 + 2 * it)
                    for i in range(2):
                        dve.bn_stats(qk_stat[:, i, :], qk[t % 2][:, i, :]).then_inc(qk_stats, 1)
                    wait_apart(dve, qk_stats, 2 * t + 2 + 4 * it)
                    dve.bn_aggr(qk_mv[t % 2][:, 0, :], qk_stat[:, 0, :])
                    dve.bn_aggr(qk_mv[t % 2][:, 1, :], qk_stat[:, 1, :]).then_inc(qk_var, 1)
                    dve.wait_ge(v_done, t + 1 + 2 * it)
                    if t == 0:
                        dve.wait_ge(ones_ready, 2)
                    if t >= 2:
                        dve.wait_ge(v_stored[t % 2], 16 * (t // 2) + 16 * it)
                    dve.tensor_scalar(v_ext[t % 2][:, :, 0:HD],
                                      ps[:, V_BANK, :].rearrange("p (h d) -> p h d", h=HEADS), CLIP, -CLIP,
                                      ALU.min, ALU.max).then_inc(v_clipped, 1)
                    dve.wait_ge(qk_dev, t + 1 + 2 * it)
                    dve.reciprocal(qk_rs[t % 2][:], qk_sd[t % 2][:]).then_inc(qk_inv, 1)
                    dve.wait_ge(qk_inv, t + 1 + 2 * it)
                    dve.tensor_scalar(qk[t % 2][:, 0, :], qk[t % 2][:, 0, :], qk_mv[t % 2][:, 0, 0:1],
                                      qk_rs[t % 2][:, 0:1], ALU.subtract, ALU.mult)
                    dve.tensor_scalar(qk[t % 2][:, 1, :], qk[t % 2][:, 1, :], qk_mv[t % 2][:, 1, 0:1],
                                      qk_rs[t % 2][:, 1:2], ALU.subtract, ALU.mult).then_inc(qk_normed, 1)

            run_tiles(dve, tile_step, -2, TILES + 1)
            dve.wait_ge(mask_ready, 2)

            def unit_step(s, it):
                n = (s + AHEAD) // NU
                if (s + AHEAD) % NU == 0 and 0 <= n < GROUPS:
                    dve.wait_ge(max_taken, NP * (n + 1) + 2 * NP * it)
                    late = max_diag[n % 2][:, :, TPB // 2:TPB]
                    dve.tensor_tensor(late, late, max_full[n % 2][:], ALU.max).then_inc(max_joined, 1)
                if s == (GROUPS - 1) * NU:
                    invert(0)
                v, n = (s + AHEAD) % NU, (s + AHEAD) // NU + 1
                if not 0 <= n < GROUPS:
                    return
                for m in sum(PLAN[v], []):
                    j, i, _, keys, diagonal = PIECES[m]
                    wait_apart(dve, max_scored, NP * n + m + 1 + 2 * NP * it)
                    scores = ps[:, MAX_BANK + m % MAX_RING, 0:keys]
                    if diagonal:
                        dve.tensor_tensor_reduce(max_junk[:, m % MAX_RING, 0:keys], scores, mask[:, BANK - keys:BANK], 1.0,
                                                 -3e38, ALU.add, ALU.max,
                                                 max_diag[n % 2][:, j, i:i + 1]).then_inc(max_taken, 1)
                    else:
                        i -= TPB // 2
                        dve.tensor_reduce(max_full[n % 2][:, j, i:i + 1], scores, AX.X,
                                          ALU.max).then_inc(max_taken, 1)

            def invert(b):
                dve.wait_ge(sums_loaded, 16 * (b + 1))
                dve.reciprocal(inv[:, b, :], sums[:, b, :]).then_inc(inverted, 1)

            run_units(dve, unit_step)

            def output_step(s, it):
                if s == 0:
                    invert(1)
                t = s + 2
                if 0 <= t < TILES:
                    dve.wait_ge(proj_done, t + 1 + 4 * it)
                    dve.wait_ge(xr_loaded[t % 4], 16 * (t // 4 + 1) + 16 * it)
                    dve.tensor_tensor(x2[t % 4][:], ps[:, O_BANK[t % 2], :], x2[t % 4][:],
                                      ALU.add).then_inc(x2_ready, 1)
                    dve.wait_ge(x2_ready, t + 1 + 4 * it)
                    dve.bn_stats(y_stat[:], x2[t % 4][:]).then_inc(y_stats, 1)
                    wait_apart(dve, y_stats, t + 1 + 4 * it)
                    dve.bn_aggr(y_mv[t % 2][:], y_stat[:]).then_inc(y_var, 1)
                if 0 <= t < TILES:
                    dve.wait_ge(y_dev, t + 1 + 4 * it)
                    dve.reciprocal(y_rs[t % 2][:], y_sd[t % 2][:]).then_inc(y_inv, 1)
                    dve.wait_ge(y_inv, t + 1 + 4 * it)
                    if t >= 2:
                        dve.wait_ge(yt_done, t - 1 + 4 * it)
                    dve.tensor_scalar(yn[t % 2][:], x2[t % 4][:], y_mv[t % 2][:, 0:1], y_rs[t % 2][:],
                                      ALU.subtract, ALU.mult).then_inc(y_normed, 1)
                t = s + 1
                if 0 <= t < TILES:
                    dve.wait_ge(yt_hi_ready, t + 1 + 4 * it)
                    dve.tensor_tensor(yt_lo[t % 2][:].rearrange("p c t -> p (c t)"), ps[:, YT_BANK[t % 2], :],
                                      yt_hi[t % 2][:].bitcast(F32).rearrange("p c t -> p (c t)"),
                                      ALU.subtract).then_inc(yt_ready, 1)
                t = s
                if 0 <= t < TILES:
                    dve.wait_ge(ff_done, t + 1 + 4 * it)
                    if t >= 2:
                        dve.wait_ge(y_stored[t % 2], 16 * (t // 2) + 32 * it)
                    dve.tensor_tensor(y_out[t % 2][:], ps[:, FF_BANK[t % 2], :], x2[t % 4][:],
                                      ALU.add).then_inc(y_ready, 1)

            run_outputs(dve, output_step)

        @block.tensor
        def _(pe):
            def product(to, hi, lo, w_hi, w_lo):
                for c in range(DC):
                    pe.matmul(to, hi[:, c, :], w_hi[:, c, :], start=(c == 0), stop=False)
                    pe.matmul(to, hi[:, c, :], w_lo[:, c, :], start=False, stop=False)
                    last = pe.matmul(to, lo[:, c, :], w_hi[:, c, :], start=False, stop=(c == DC - 1))
                return last

            def turn(bank, rows):
                for c in range(DC):
                    last = pe.transpose(ps[:, bank, c * P:(c + 1) * P], rows[:, c * P:(c + 1) * P], ident[:])
                return last

            pe.wait_ge(ident_ready, 2)

            def tile_step(s, it):
                t = s + 1
                if 0 <= t < TILES:
                    pe.wait_ge(x_normed, t + 1 + 2 * it)
                    if t >= 1:
                        pe.wait_ge(xt_ready, t + 2 * it)
                    turn(XT_BANK, xn[t % 2]).then_inc(xt_done, 1)
                t = s
                if 0 <= t < TILES:
                    if t == 0:
                        pe.wait_ge(wqkv_ready, DC)
                    pe.wait_ge(xt_ready, t + 1 + 2 * it)
                    if t >= 2:
                        pe.wait_ge(qk_clipped, t - 1 + 2 * it)
                    for i in range(2):
                        last = product(ps[:, QK_BANK[t % 2] + i, :], xt_hi[t % 2], xt_lo[t % 2],
                                       wqkv_hi[:, :, i * D:(i + 1) * D], wqkv_lo[:, :, i * D:(i + 1) * D])
                    last.then_inc(qk_done, 1)
                    if t >= 1:
                        pe.wait_ge(v_clipped, t + 2 * it)
                    product(ps[:, V_BANK, :], xt_hi[t % 2], xt_lo[t % 2],
                            wqkv_hi[:, :, 2 * D:3 * D], wqkv_lo[:, :, 2 * D:3 * D]).then_inc(v_done, 1)
                t = s - 1
                if 0 <= t < TILES:
                    pe.wait_ge(qk_ready, t + 1 + 2 * it)
                    if t >= 1:
                        pe.wait_ge(rest_ready, t + 2 * it)
                    turn(QKT_BANK, qk[t % 2][:, 0, :])
                    turn(QKT_BANK + 1, qk[t % 2][:, 1, :]).then_inc(qkt_done, 1)

            run_tiles(pe, tile_step, -1, TILES)
            pe.wait_ge(mask_ready, 2)
            pe.wait_ge(rest_ready, TILES)
            pe.wait_ge(v_clipped, TILES)

            def unit_step(s, it):
                v, n_max = (s + AHEAD) % NU, (s + AHEAD) // NU + 1

                def max_pieces_of(slot):
                    if not 0 <= n_max < GROUPS:
                        return
                    for m in PLAN[v][slot]:
                        j, i, key, keys, _ = PIECES[m]
                        if m == 0:
                            pe.wait_ge(max_loaded[n_max % 2], 128 * (n_max // 2 + 1) + 128 * it)
                        if m == TURN_SLOT and n_max >= 1:
                            pe.wait_ge(shift_hi_ready, 2 * n_max + 4 * it)
                        if NP * n_max + m >= MAX_RING:
                            pe.wait_ge(max_taken, NP * n_max + m - MAX_RING + 1 + 2 * NP * it)
                        rows = MAX_K + BIAS_ROWS
                        pe.matmul(ps[:, MAX_BANK + m % MAX_RING, 0:keys],
                                  max_q[n_max % 2][0:rows, j, i * P:(i + 1) * P],
                                  max_k[n_max % 2][0:rows, j, key:key + keys],
                                  start=True, stop=True).then_inc(max_scored, 1)

                def score(pair):
                    u, n = s % NU, s // NU
                    first_q, cols = unit_columns(u)
                    kb = UNITS[u][1]
                    rows = EXP_K + BIAS_ROWS + SHIFT_ROWS
                    if u == 0 and pair == 0:
                        pe.wait_ge(exp_loaded[n % 2], 224 * (n // 2 + 1) + 224 * it)
                        pe.wait_ge(shift_loaded[n % 2], 32 * (n // 2 + 1) + 32 * it)
                    if s >= 1:
                        pe.wait_ge(exp_done, 2 * s - 1 + pair + 4 * NU * it)
                    for j in range(2):
                        last = pe.matmul(ps[:, EXP_BANK[pair] + j, 0:cols],
                                         exp_k[n % 2][0:rows, 2 * pair + j, kb * P:(kb + 1) * P],
                                         exp_q[n % 2][0:rows, 2 * pair + j, first_q:first_q + cols],
                                         start=True, stop=not is_diagonal(u))
                        if is_diagonal(u):
                            last = pe.matmul(ps[:, EXP_BANK[pair] + j, 0:P], ident_half[:], mask_turned[:],
                                             start=False, stop=True)
                    last.then_inc(scored, 1)

                if 0 <= s < GROUPS * NU:
                    score(0)
                max_pieces_of(0)
                w = s - LAG
                if 0 <= w < GROUPS * NU:
                    u, n = w % NU, w // NU
                    half, kb = UNITS[u]
                    first_q, cols = unit_columns(u)
                    if u == 0:
                        pe.wait_ge(v_loaded[n % 2], 16 * (n // 2 + 1) + 16 * it)
                    if kb == 0 and 2 * n + half >= 1:
                        pe.wait_ge(o_ready, 2 * n + half + 4 * it)
                    pe.wait_ge(exp_done, 2 * (w + 1) + 4 * NU * it)
                    to = first_q - half * BANK
                    last_kb = (half + 1) * TPB // 2 - 1
                    for j in range(G):
                        last = pe.matmul(ps[j * VW:(j + 1) * VW, PV_BANK, to:to + cols],
                                         v_sb[n % 2][:, kb, j * VW:(j + 1) * VW],
                                         probs[w % P_SLOTS][:, j, 0:cols],
                                         start=(kb == 0), stop=(kb == last_kb))
                    last.then_inc(pv_done, 1)
                max_pieces_of(1)
                n = n_max - 1
                if v == 0 and 0 <= n < GROUPS:
                    pe.wait_ge(max_joined, n + 1 + 2 * it)
                    pe.transpose(ps[0:G * TPB, MAX_BANK + TURN_SLOT, 0:P],
                                 max_diag[n % 2][:].rearrange("p j i -> p (j i)"), ident[:]).then_inc(max_turned, 1)
                if 0 <= s < GROUPS * NU:
                    score(1)
                max_pieces_of(2)

            run_units(pe, unit_step)
            pe.wait_ge(o_ready, 2 * GROUPS)

            def output_step(s, it):
                t = s + 2
                if 0 <= t < TILES:
                    if t == 0:
                        pe.wait_ge(wout_ready, DC)
                    pe.wait_ge(att_lo_ready, t + 1 + 4 * it)
                    if t >= 2:
                        pe.wait_ge(x2_ready, t - 1 + 4 * it)
                    product(ps[:, O_BANK[t % 2], :], att_hi[t % 2], att_lo[t % 2],
                            wout_hi, wout_lo).then_inc(proj_done, 1)
                t = s + 1
                if 0 <= t < TILES:
                    pe.wait_ge(y_normed, t + 1 + 4 * it)
                    if t >= 2:
                        pe.wait_ge(yt_ready, t - 1 + 4 * it)
                    turn(YT_BANK[t % 2], yn[t % 2]).then_inc(yt_done, 1)
                t = s
                if 0 <= t < TILES:
                    if t == 0:
                        pe.wait_ge(wffn_ready, DC)
                    pe.wait_ge(yt_ready, t + 1 + 4 * it)
                    if t >= 2:
                        pe.wait_ge(y_ready, t - 1 + 4 * it)
                    product(ps[:, FF_BANK[t % 2], :], yt_hi[t % 2], yt_lo[t % 2],
                            wffn_hi, wffn_lo).then_inc(ff_done, 1)

            run_outputs(pe, output_step)


def alibi_rows(bf16):
    steps = np.arange(1, HEADS + 1, dtype=np.float32) * (ALIBI_MAX / HEADS)
    slopes = (1.0 / np.power(2.0, steps)).astype(np.float32)
    bias = slopes[:, None].astype(np.float64) * np.arange(SEQ) / SCALE
    rows = np.ones((2, BIAS_ROWS + SHIFT_ROWS, HEADS, SEQ), dtype=bf16)
    for n in range(3):
        part = bias.astype(np.float32).astype(bf16)
        bias = bias - part.astype(np.float64)
        rows[1, 2 * n] = part
        rows[0, 2 * n + 1] = -part
    return rows


def kernel(L0_attn_hidden_states, L0_attn_Wqkv, L0_attn_q_ln_w, L0_attn_q_ln_b, L0_attn_k_ln_w,
           L0_attn_k_ln_b, L0_attn_Wout, L0_ffn_bases, L0_ffn_alphas):
    import ml_dtypes
    import concourse.bacc as bacc
    from concourse.bass_utils import run_bass_kernel_spmd

    x = np.asarray(L0_attn_hidden_states)
    arrays = {
        "x": np.ascontiguousarray(x.reshape(TILES, P, D)),
        "wqkv_t": np.ascontiguousarray(np.asarray(L0_attn_Wqkv).T),
        "qk_w": np.stack([np.asarray(L0_attn_q_ln_w), np.asarray(L0_attn_k_ln_w)]),
        "qk_b": np.stack([np.asarray(L0_attn_q_ln_b), np.asarray(L0_attn_k_ln_b)]),
        "wout_t": np.ascontiguousarray(np.asarray(L0_attn_Wout).reshape(D, HEADS, HD).transpose(2, 1, 0).reshape(D, D)),
        "bases_t": np.ascontiguousarray(np.asarray(L0_ffn_bases).transpose(0, 2, 1)),
        "alphas": np.ascontiguousarray(np.asarray(L0_ffn_alphas)[:, :, 0]),
        "bias_rows": alibi_rows(ml_dtypes.bfloat16),
    }
    nc = bacc.Bacc("TRN2", target_bir_lowering=False, num_devices=1)
    args = [nc.dram_tensor(f"in_{k}", a.shape, mybir.dt.from_np(a.dtype), kind="ExternalInput").ap()
            for k, a in arrays.items()]
    out = nc.dram_tensor("out", (TILES, P, D), F32, kind="ExternalOutput").ap()
    build(nc, *args, out)
    r = run_bass_kernel_spmd(nc, [{f"in_{k}": a for k, a in arrays.items()}], core_ids=[0])
    return r.results[0]["out"].reshape(x.shape)
```

```python
from contextlib import ExitStack

import numpy as np

import concourse.bass as bass
from concourse import mybir

F32 = mybir.dt.float32
F32R = mybir.dt.float32r
BF16 = mybir.dt.bfloat16
ALU = mybir.AluOpType
ACT = mybir.ActivationFunctionType
AX = mybir.AxisListType
ds = bass.ds

P = 128
BANK = 512
D = 512
DC = D // P
BATCH, SEQ = 2, 1024
TILES = BATCH * SEQ // P
TPB = SEQ // P
HEADS, HD = 32, 16
G = 4
GROUPS = BATCH * HEADS // G
GPB = HEADS // G
VW = 32
CLIP = 8.0
EPS = 1e-5
SCALE = HD ** -0.5
ALIBI_MAX = 8.0
MASKED = -1e30

TERMS = [(0, 0), (0, 1), (1, 0), (1, 1), (0, 2), (2, 0)]
MAX_TERMS = 3
BIAS_ROWS = 6
SHIFT_ROWS = 2
EXP_K = len(TERMS) * HD
MAX_K = MAX_TERMS * HD

UNITS = [(h, kb) for h in range(2) for kb in range((h + 1) * TPB // 2)]
NU = len(UNITS)
LAG = 2
AHEAD = 4
P_SLOTS = 3
MAX_RING = 3
TURN_SLOT = 2


def unit_columns(u):
    half, kb = UNITS[u]
    first = max(kb * P, half * BANK)
    return first, (half + 1) * BANK - first


def is_diagonal(u):
    half, kb = UNITS[u]
    return kb * P >= half * BANK


def max_pieces():
    out = []
    for j in range(G):
        for i in reversed(range(TPB)):
            keys = (i + 1) * P
            if keys > BANK:
                out.append((j, i, 0, BANK, False))
                out.append((j, i, BANK, keys - BANK, True))
            else:
                out.append((j, i, 0, keys, True))
    return out


PIECES = max_pieces()
NP = len(PIECES)
assert NP % MAX_RING == 0 and (2 * NU) % P_SLOTS == 0


SLOTS = 3
LEAD = 3 * P


def piece_plan():
    slots = []
    for v in range(NU):
        u, w = (v + NU - AHEAD) % NU, (v + 2 * NU - AHEAD - LAG) % NU
        qk_cols = 2 * (unit_columns(u)[1] + (P if is_diagonal(u) else 0))
        slots += [qk_cols, 4 * unit_columns(w)[1], qk_cols]
    total, pe_all, at = sum(n for _, _, _, n, _ in PIECES), sum(slots), 0
    plan, pe_time, done = [], 0, 0
    for k, cols in enumerate(slots):
        pe_time += cols
        mine = []
        while at < NP and (at == k if k < 2 else k >= SLOTS and done + PIECES[at][3] / 2 - LEAD <= pe_time * total / pe_all
                           or k == len(slots) - 1):
            mine.append(at)
            done += PIECES[at][3]
            at += 1
            if k < 2:
                break
        plan.append(mine)
    return [plan[SLOTS * v:SLOTS * (v + 1)] for v in range(NU)]


PLAN = piece_plan()

FIRST_UNIT = -NU - AHEAD
EARLY_UNITS = 3

STACKS_AT = 14
assert STACKS_AT - 2 >= TPB and STACKS_AT % 4 == 2
WEIGHTS_AT = [8, 10, 12, 14] + [(GROUPS - 2) * NU + v for v in (0, 2, 4, 6)]


def build(nc, x, wqkv_t, qk_w, qk_b, wout_t, bases_t, alphas, bias_rows, out):
    ctx = ExitStack()

    def alloc(stack):
        def sb(name, shape, dt=F32):
            return stack.enter_context(nc.sbuf_tensor(name, shape, dt))
        return sb

    def sem(name):
        return ctx.enter_context(nc.semaphore(name))

    parts_dram = nc.dram_tensor("parts_dram", [2, 3, BATCH, D, SEQ], BF16).ap()
    v_dram = nc.dram_tensor("v_dram", [BATCH, GPB, TPB, P, G * VW], F32).ap()
    o_dram = nc.dram_tensor("o_dram", [BATCH, VW, HEADS, SEQ], F32).ap()
    inv_dram = nc.dram_tensor("inv_dram", [BATCH, HEADS, SEQ], F32).ap()

    with ctx:
        sb = alloc(ctx)
        ident = sb("ident", [P, P])
        ident_half = sb("ident_half", [P, P], BF16)
        mask = sb("mask", [P, BANK], BF16)
        mask_turned = sb("mask_turned", [P, P], BF16)
        eps = sb("eps", [P, 1])
        wout_hi = sb("wout_hi", [P, DC, D], F32R)
        wout_lo = sb("wout_lo", [P, DC, D], F32R)
        wffn_hi = sb("wffn_hi", [P, DC, D], F32R)
        wffn_lo = sb("wffn_lo", [P, DC, D], F32R)
        wffn_term = sb("wffn_term", [P, 2, D])

        with ExitStack() as staging:
            sb = alloc(staging)
            parts_second = sb("parts1", [P, 3, 2, DC, 2 * P], BF16)
            wqkv_raw = sb("wqkv_raw", [P, DC, 3 * D])
        sb = alloc(ctx)
        exp_q_odd, exp_k_odd = (sb(f"{name}1", [P, G, SEQ], BF16) for name in ("exp_q", "exp_k"))
        exp_q = [sb("exp_q0", [P, G, SEQ], BF16), exp_q_odd]
        exp_k = [sb("exp_k0", [P, G, SEQ], BF16), exp_k_odd]
        max_q = [sb(f"max_q{i}", [P, G, SEQ], BF16) for i in range(2)]
        max_k = [sb(f"max_k{i}", [P, G, SEQ], BF16) for i in range(2)]

        with ExitStack() as first:
            sb = alloc(first)
            wqkv_hi = sb("wqkv_hi", [P, DC, 3 * D], F32R)
            wqkv_lo = sb("wqkv_lo", [P, DC, 3 * D], F32R)
            qk_gain = sb("qk_gain", [P, 2, D])
            qk_bias = sb("qk_bias", [P, 2, D])
            x_in = [sb(f"x_in{i}", [P, D]) for i in range(2)]
            xn = [sb(f"xn{i}", [P, D]) for i in range(2)]
            xt_hi = [sb(f"xt_hi{i}", [P, DC, P], F32R) for i in range(2)]
            xt_lo = [sb(f"xt_lo{i}", [P, DC, P], F32R) for i in range(2)]
            qk = [sb(f"qk{i}", [P, 2, D]) for i in range(2)]
            v_ext = [sb(f"v_ext{i}", [P, HEADS, VW]) for i in range(2)]
            rest = sb("rest", [P, 2, DC, P])
            parts = [sb("parts0", [P, 3, 2, DC, 2 * P], BF16), parts_second]
            x_stat = sb("x_stat", [P, 6])
            x_mv = [sb(f"x_mv{i}", [P, 2]) for i in range(2)]
            x_sd = [sb(f"x_sd{i}", [P, 1]) for i in range(2)]
            x_rs = [sb(f"x_rs{i}", [P, 1]) for i in range(2)]
            qk_stat = sb("qk_stat", [P, 2, 6])
            qk_mv = [sb(f"qk_mv{i}", [P, 2, 2]) for i in range(2)]
            qk_sd = [sb(f"qk_sd{i}", [P, 2]) for i in range(2)]
            qk_rs = [sb(f"qk_rs{i}", [P, 2]) for i in range(2)]
        sb = alloc(ctx)
        probs = [sb(f"probs{i}", [P, G, BANK]) for i in range(P_SLOTS)]
        v_sb = [sb(f"v_sb{i}", [P, TPB, G * VW]) for i in range(2)]
        o_sb = [sb(f"o_sb{i}", [P, BANK]) for i in range(2)]
        max_junk = sb("max_junk", [P, MAX_RING, BANK], BF16)
        max_diag = [sb(f"max_diag{i}", [P, G, TPB]) for i in range(2)]
        max_full = [sb(f"max_full{i}", [P, G, TPB // 2]) for i in range(2)]
        shift = [sb(f"shift{i}", [G * TPB, P]) for i in range(2)]
        shift_hi = [sb(f"shift_hi{i}", [G * TPB, P], BF16) for i in range(2)]
        shift_mid = [sb(f"shift_mid{i}", [G * TPB, P], BF16) for i in range(2)]
        with ExitStack() as staging:
            sb = alloc(staging)
            wout_raw = sb("wout_raw", [P, DC, D])
            bases_sb = sb("bases_sb", [P, 4, DC, D], BF16)
            alpha_sb = sb("alpha_sb", [P, 4, D])
            wffn_sum = sb("wffn_sum", [P, DC, D])
        sb = alloc(ctx)
        o_in = [sb(f"o_in{i}", [P, DC, P]) for i in range(2)]
        inv_in = [sb(f"inv_in{i}", [P, P]) for i in range(2)]
        sums = sb("sums", [P, BATCH, HEADS * SEQ // P])
        inv = sb("inv", [P, BATCH, HEADS * SEQ // P])
        att = [sb(f"att{i}", [P, DC, P]) for i in range(2)]
        att_hi = [sb(f"att_hi{i}", [P, DC, P], F32R) for i in range(2)]
        att_lo = [sb(f"att_lo{i}", [P, DC, P], F32R) for i in range(2)]
        x2 = [sb(f"x2_{i}", [P, D]) for i in range(4)]
        yn = [sb(f"yn{i}", [P, D]) for i in range(2)]
        yt_hi = [sb(f"yt_hi{i}", [P, DC, P], F32R) for i in range(2)]
        yt_lo = [sb(f"yt_lo{i}", [P, DC, P], F32R) for i in range(2)]
        y_out = [sb(f"y_out{i}", [P, D]) for i in range(2)]
        y_stat = sb("y_stat", [P, 6])
        y_mv = [sb(f"y_mv{i}", [P, 2]) for i in range(2)]
        y_sd = [sb(f"y_sd{i}", [P, 1]) for i in range(2)]
        y_rs = [sb(f"y_rs{i}", [P, 1]) for i in range(2)]

        ps = ctx.enter_context(nc.psum_tensor("ps", [P, 8, BANK], F32))
        XT_BANK, QK_BANK, V_BANK, QKT_BANK = 0, (1, 3), 5, 6
        EXP_BANK, PV_BANK, MAX_BANK = (4, 6), 3, 0
        O_BANK, YT_BANK, FF_BANK = (0, 1), (2, 3), (4, 5)

        ident_zero, ident_ready, mask_zero, mask_ready = (
            sem("ident_zero"), sem("ident_ready"), sem("mask_zero"), sem("mask_ready"))
        eps_ready, ones_ready = sem("eps_ready"), sem("ones_ready")
        wqkv_loaded = [sem(f"w{n}_loaded") for n in "qkv"]
        gain_loaded, wout_loaded, bases_loaded, alphas_loaded = (
            sem("gain_loaded"), sem("wout_loaded"), sem("bases_loaded"), sem("alphas_loaded"))
        wqkv_hi_ready, wqkv_ready = sem("wqkv_hi_ready"), sem("wqkv_ready")
        wout_hi_ready, wout_ready = sem("wout_hi_ready"), sem("wout_ready")
        wffn_term_ready, wffn_summed = sem("wffn_term_ready"), sem("wffn_summed")
        wffn_hi_ready, wffn_ready = sem("wffn_hi_ready"), sem("wffn_ready")
        waits_passed = [sem("waits_passed_dve"), sem("waits_passed_pool")]
        x_loaded = [sem(f"x_loaded{i}") for i in range(2)]
        x_stats, x_var, x_dev, x_inv, x_normed = (
            sem("x_stats"), sem("x_var"), sem("x_dev"), sem("x_inv"), sem("x_normed"))
        xt_done, xt_hi_ready, xt_ready = sem("xt_done"), sem("xt_hi_ready"), sem("xt_ready")
        qk_done, v_done = sem("qk_done"), sem("v_done")
        qk_clipped, v_clipped = sem("qk_clipped"), sem("v_clipped")
        qk_stats, qk_var, qk_dev, qk_inv, qk_normed = (
            sem("qk_stats"), sem("qk_var"), sem("qk_dev"), sem("qk_inv"), sem("qk_normed"))
        qk_scaled, qk_ready = sem("qk_scaled"), sem("qk_ready")
        qkt_done, hi_ready, rest_ready, mid_ready, lo_ready = (
            sem("qkt_done"), sem("hi_ready"), sem("rest_ready"), sem("mid_ready"), sem("lo_ready"))
        v_stored = [sem(f"v_stored{i}") for i in range(2)]
        parts_stored = [sem(f"parts_stored{i}") for i in range(2)]
        max_loaded = [sem(f"max_loaded{i}") for i in range(2)]
        exp_loaded = [sem(f"exp_loaded{i}") for i in range(2)]
        v_loaded = [sem(f"v_loaded{i}") for i in range(2)]
        shift_loaded = [sem(f"shift_loaded{i}") for i in range(2)]
        max_scored, max_taken, max_joined, max_turned = (
            sem("max_scored"), sem("max_taken"), sem("max_joined"), sem("max_turned"))
        shift_hi_ready, shift_ready = sem("shift_hi_ready"), sem("shift_ready")
        scored, exp_done, pv_done, o_ready = (
            sem("scored"), sem("exp_done"), sem("pv_done"), sem("o_ready"))
        o_stored = [sem(f"o_stored{i}") for i in range(2)]
        o_loaded = [sem(f"o_loaded{i}") for i in range(2)]
        xr_loaded = [sem(f"xr_loaded{i}") for i in range(4)]
        sums_loaded, inverted, inv_stored = sem("sums_loaded"), sem("inverted"), sem("inv_stored")
        att_ready, att_hi_ready, att_lo_ready = (
            sem("att_ready"), sem("att_hi_ready"), sem("att_lo_ready"))
        proj_done, x2_ready = sem("proj_done"), sem("x2_ready")
        y_stats, y_var, y_dev, y_inv, y_normed = (
            sem("y_stats"), sem("y_var"), sem("y_dev"), sem("y_inv"), sem("y_normed"))
        yt_done, yt_hi_ready, yt_ready = sem("yt_done"), sem("yt_hi_ready"), sem("yt_ready")
        ff_done, y_ready = sem("ff_done"), sem("y_ready")
        y_stored = [sem(f"y_stored{i}") for i in range(2)]

        block = ctx.enter_context(nc.Block())

        def run(eng, step, first, last, body, loop_first, rounds):
            for s in range(first, loop_first):
                step(s, 0)
            with eng.Fori(0, rounds) as it:
                for s in range(loop_first, loop_first + body):
                    step(s, it)
            for s in range(loop_first + body * rounds, last + 1):
                step(s, 0)

        def wait_apart(eng, semaphore, value):
            eng.wait_ge(semaphore, value)
            eng.sem_inc(waits_passed[eng is nc.gpsimd], 1)

        def run_tiles(eng, step, first, last):
            run(eng, step, first, last, 4, 5, 2)

        def run_units(eng, step, first=FIRST_UNIT):
            run(eng, step, first, GROUPS * NU + LAG - 1, 2 * NU, NU + LAG + 1, GROUPS // 2 - 2)

        def run_groups(eng, step):
            run(eng, step, -2, GROUPS, 2, 1, GROUPS // 2 - 2)

        def run_outputs(eng, step):
            run(eng, step, -4, TILES - 1, 4, 2, 2)

        @block.sync
        def _(sp):
            sp.dma_start(x_in[0][:], x[0]).then_inc(x_loaded[0], 16)
            for i in range(3):
                sp.dma_start(wqkv_raw[:, :, i * D:(i + 1) * D],
                             wqkv_t[:, i * D:(i + 1) * D].rearrange("(c p) o -> p c o", p=P)
                             ).then_inc(wqkv_loaded[i], 16)
                if i == 0:
                    sp.dma_start(x_in[1][:], x[1]).then_inc(x_loaded[1], 16)
            for i in range(2):
                sp.dma_start(qk_gain[:, i, :], qk_w[i:i + 1, :].partition_broadcast(P)).then_inc(gain_loaded, 16)
                sp.dma_start(qk_bias[:, i, :], qk_b[i:i + 1, :].partition_broadcast(P)).then_inc(gain_loaded, 16)

            def tile_step(s, it):
                t = s + 3
                if 2 <= t < TILES:
                    sp.wait_ge(x_normed, t - 1 + 4 * it)
                    sp.dma_start(x_in[t % 2][:], x[t + 4 * it]).then_inc(x_loaded[t % 2], 16)
                t = s
                if 0 <= t < TILES:
                    sp.wait_ge(v_clipped, t + 1 + 4 * it)
                    tt = t + 4 * it
                    sp.dma_start(v_dram[tt // TPB, :, tt % TPB, :, :].rearrange("g p n -> p g n"),
                                 v_ext[t % 2][:].rearrange("p (g h) n -> p g (h n)", g=GPB)
                                 ).then_inc(v_stored[t % 2], 16)
                t = s - 2
                if 0 <= t < TILES and t % 2:
                    sp.wait_ge(lo_ready, t + 1 + 4 * it)
                    sp.wait_ge(mid_ready, t + 1 + 4 * it)
                    tt = t - 1 + 4 * it
                    for n in range(3):
                        for i in range(2):
                            sp.dma_start(
                                parts_dram[i, n, tt // TPB, :, ds((tt % TPB) * P, 2 * P)]
                                .rearrange("(c p) t -> p c t", p=P),
                                parts[t // 2 % 2][:, n, i, :, :]).then_inc(parts_stored[t // 2 % 2], 16)

            def projections_over():
                for i in range(2):
                    sp.wait_ge(parts_stored[i], 6 * 16 * TILES // 4)
                    sp.wait_ge(v_stored[i], 16 * TILES // 2)
                sp.wait_ge(qkt_done, TILES)
                sp.wait_ge(lo_ready, TILES)

            def load_last_weights():
                for k in range(4):
                    sp.dma_start(alpha_sb[:, k, :], alphas[k:k + 1, :].partition_broadcast(P)).then_inc(alphas_loaded, 16)
                sp.dma_start(wout_raw[:], wout_t.rearrange("(c p) o -> p c o", p=P)).then_inc(wout_loaded, 16)

            def stack(dst_q, dst_k, terms, n, it, loaded):
                nn = n + 2 * it
                for i, dst in ((0, dst_q), (1, dst_k)):
                    for r, term in enumerate(terms):
                        src = parts_dram[i, term[i]].rearrange("b f t -> (b f) t")
                        sp.dma_start(dst[r * HD:(r + 1) * HD, :, :],
                                     src[ds(nn * (G * HD), G * HD), :].rearrange("(j d) t -> d j t", j=G)
                                     ).then_inc(loaded, 16)
                    r = len(terms) * HD
                    rows = BIAS_ROWS + (SHIFT_ROWS if i == 1 and len(terms) > MAX_TERMS else 0)
                    sp.dma_start(dst[r:r + rows, :, :],
                                 bias_rows[i, 0:rows, ds((nn % GPB) * G, G), :]).then_inc(loaded, 16)

            def tile_step_and_stacks(s, it):
                tile_step(s, it)
                if s == STACKS_AT:
                    for i in range(2):
                        sp.wait_ge(parts_stored[i], 6 * 16 * (STACKS_AT - 2) // 4)
                    sp.wait_ge(wqkv_ready, 3 * DC)
                    for n in range(2):
                        load_max(n, 0)
                    load_exp(0, 0)

            def load_max(n, it):
                stack(max_q[n % 2], max_k[n % 2], TERMS[:MAX_TERMS], n, it, max_loaded[n % 2])

            def load_exp(n, it):
                stack(exp_q[n % 2], exp_k[n % 2], TERMS, n, it, exp_loaded[n % 2])

            run_tiles(sp, tile_step_and_stacks, -1, TILES + 1)
            projections_over()

            def group_step(s, it):
                n = s + 2
                if 2 <= n < GROUPS:
                    sp.wait_ge(max_scored, NP * (n - 1) + 2 * NP * it)
                    load_max(n, it)
                n = s + 1
                if 0 <= n < GROUPS:
                    if n >= 2:
                        sp.wait_ge(scored, 2 * NU * (n - 1) + 4 * NU * it)
                    if n >= 1:
                        load_exp(n, it)
                    if n >= 2:
                        sp.wait_ge(pv_done, NU * (n - 1) + 2 * NU * it)
                    nn = n + 2 * it
                    sp.dma_start(v_sb[n % 2][:], v_dram.rearrange("b g k p n -> (b g) k p n")[nn]
                                 .rearrange("k p n -> p k n")).then_inc(v_loaded[n % 2], 16)
                if s == 0:
                    load_last_weights()
                for n, half in ((s - 1, 1), (s, 0)):
                    if 0 <= n < GROUPS:
                        sp.wait_ge(o_ready, 2 * n + half + 1 + 4 * it)
                        nn = n + 2 * it
                        sp.dma_start(o_dram[nn // GPB, :, ds((nn % GPB) * G, G), half * BANK:(half + 1) * BANK]
                                     .rearrange("r j t -> j r t"), o_sb[half][:]).then_inc(o_stored[half], 16)
                n = s + 1
                if 0 <= n < GROUPS:
                    sp.wait_ge(shift_ready, n + 1 + 2 * it)
                    for r, part in ((0, shift_hi), (1, shift_mid)):
                        row = EXP_K + BIAS_ROWS + r
                        sp.dma_start(exp_q[n % 2][row:row + 1, :, :].rearrange("p j t -> p (j t)"),
                                     part[n % 2][:]).then_inc(shift_loaded[n % 2], 16)

                if s == GROUPS - 2:
                    load_sums(0)
                if s == GROUPS - 1:
                    store_inverses(0)
                    sp.wait_ge(inv_stored, 16)
                    sp.wait_ge(wout_ready, DC)
                    sp.wait_ge(wffn_ready, DC)
                    for t in range(3):
                        if t == 2:
                            sp.wait_ge(att_ready, 1)
                        load_sums_of_tile(t, 0)
                        load_residual(t, 0)

            def load_sums_of_tile(t, it):
                tt = t + 4 * it
                sp.dma_start(o_in[t % 2][:], o_dram[tt // TPB, 0:HD, :, ds((tt % TPB) * P, P)]
                             .rearrange("(c r) h t -> (r h) c t", c=DC)).then_inc(o_loaded[t % 2], 16)
                rows = inv_dram[tt // TPB, :, ds((tt % TPB) * P, P)]
                sp.dma_start(inv_in[t % 2][:], rows.rearrange("(a h) t -> a h t", a=1)
                             .broadcast_to([HD // DC, HEADS, P])).then_inc(o_loaded[t % 2], 16)

            def load_residual(t, it):
                sp.dma_start(x2[t % 4][:], x[t + 4 * it]).then_inc(xr_loaded[t % 4], 16)

            def load_sums(b):
                for half in range(2):
                    sp.wait_ge(o_stored[half], 16 * (GROUPS if b else GROUPS - 1 - half))
                sp.dma_start(sums[:, b, :], o_dram[b, HD].rearrange("h (q t) -> (h q) t", q=P // HEADS)
                             ).then_inc(sums_loaded, 16)

            def store_inverses(b):
                sp.wait_ge(inverted, b + 1)
                sp.dma_start(inv_dram[b].rearrange("h (q t) -> (h q) t", q=P // HEADS),
                             inv[:, b, :]).then_inc(inv_stored, 16)

            run_groups(sp, group_step)

            def output_step(s, it):
                t = s + 4
                if 3 <= t < TILES:
                    sp.wait_ge(att_ready, t - 1 + 4 * it)
                    load_sums_of_tile(t, it)
                t = s + 3
                if 3 <= t < TILES:
                    if t >= 4:
                        sp.wait_ge(y_ready, t - 3 + 4 * it)
                    load_residual(t, it)
                t = s
                if 0 <= t < TILES:
                    sp.wait_ge(y_ready, t + 1 + 4 * it)
                    sp.dma_start(out[t + 4 * it], y_out[t % 2][:]).then_inc(y_stored[t % 2], 16)
                if s == -1:
                    load_sums(1)
                if s == 0:
                    store_inverses(1)
                if s == 1:
                    sp.wait_ge(inv_stored, 16 * BATCH)

            run_outputs(sp, output_step)
            for i in range(2):
                sp.wait_ge(y_stored[i], 16 * TILES // 2)

        @block.gpsimd
        def _(pool):
            pool.memset(eps[:], EPS).then_inc(eps_ready, 1)
            pool.memset(ident[:], 0.0).then_inc(ident_zero, 1)
            pool.wait_ge(ident_zero, 1)
            pool.affine_select(out=ident[:], in_=ident[:], compare_op=ALU.not_equal, fill=1.0, base=0,
                               pattern=[[-1, P]], channel_multiplier=1).then_inc(ident_ready, 1)
            pool.memset(ident_half[:], 0.0).then_inc(ident_zero, 1)
            pool.wait_ge(ident_zero, 2)
            pool.affine_select(out=ident_half[:], in_=ident_half[:], compare_op=ALU.not_equal, fill=1.0, base=0,
                               pattern=[[-1, P]], channel_multiplier=1).then_inc(ident_ready, 1)
            pool.memset(mask_turned[:], 0.0).then_inc(mask_zero, 1)
            pool.wait_ge(mask_zero, 1)
            pool.affine_select(out=mask_turned[:], in_=mask_turned[:], compare_op=ALU.is_ge, fill=MASKED, base=0,
                               pattern=[[1, P]], channel_multiplier=-1).then_inc(mask_ready, 1)
            pool.memset(mask[:], 0.0).then_inc(mask_zero, 1)
            pool.wait_ge(mask_zero, 2)
            pool.affine_select(out=mask[:], in_=mask[:], compare_op=ALU.is_ge, fill=MASKED, base=BANK - P,
                               pattern=[[-1, BANK]], channel_multiplier=1).then_inc(mask_ready, 1)
            for i in range(2):
                pool.memset(v_ext[i][:], 1.0).then_inc(ones_ready, 1)

            def low_part(lo, whole, hi, hi_ready_, ready):
                for c in range(DC):
                    pool.wait_ge(hi_ready_, c + 1)
                    pool.tensor_tensor(lo[:, c, :], whole[:, c, :], hi[:, c, :].bitcast(F32),
                                       ALU.subtract).then_inc(ready, 1)

            def tile_step(s, it):
                t = s - 2
                if 0 <= t < TILES:
                    pool.wait_ge(mid_ready, t + 1 + 4 * it)
                    half = ds((t % 2) * P, P)
                    pair = parts[t // 2 % 2]
                    pool.tensor_tensor(pair[:, 2, :, :, half], rest[:], pair[:, 1, :, :, half],
                                       ALU.subtract).then_inc(lo_ready, 1)
                t = s
                if 0 <= t < TILES:
                    if t == 0:
                        pool.wait_ge(gain_loaded, 4 * 16)
                    pool.wait_ge(qk_normed, t + 1 + 4 * it)
                    pool.tensor_tensor(qk[t % 2][:], qk[t % 2][:], qk_gain[:], ALU.mult).then_inc(qk_scaled, 1)
                    pool.wait_ge(qk_scaled, t + 1 + 4 * it)
                    pool.tensor_tensor(qk[t % 2][:], qk[t % 2][:], qk_bias[:], ALU.add).then_inc(qk_ready, 1)

            run_tiles(pool, tile_step, 0, TILES + 1)

            def load_bases():
                pool.wait_ge(v_loaded[0], 16)
                for k in range(4):
                    pool.dma_start(bases_sb[:, k, :, :],
                                   bases_t[k].rearrange("(c p) o -> p c o", p=P)).then_inc(bases_loaded, 16)
                pool.wait_ge(bases_loaded, 4 * 16)
                pool.wait_ge(alphas_loaded, 4 * 16)

            def sum_bases(c):
                for k in range(4):
                    to = wffn_sum[:, c, :] if k == 0 else wffn_term[:, k % 2, :]
                    done = 3 * c + max(k - 1, 0)
                    if done:
                        pool.wait_ge(wffn_summed, done)
                    pool.tensor_tensor(to, bases_sb[:, k, c, :], alpha_sb[:, k, :],
                                       ALU.mult).then_inc(wffn_term_ready, 1)
                    if k:
                        pool.wait_ge(wffn_term_ready, 4 * c + k + 1)
                        if done:
                            pool.wait_ge(wffn_summed, done)
                        pool.tensor_tensor(wffn_sum[:, c, :], wffn_sum[:, c, :], wffn_term[:, k % 2, :],
                                           ALU.add).then_inc(wffn_summed, 1)

            def unit_step(s, it):
                n = (s + AHEAD) // NU
                if (s + AHEAD) % NU == 0 and 0 <= n < GROUPS:
                    pool.wait_ge(shift_hi_ready, 2 * (n + 1) + 4 * it)
                    pool.tensor_tensor(shift_mid[n % 2][:], shift[n % 2][:], shift_hi[n % 2][:],
                                       ALU.subtract).then_inc(shift_ready, 1)
                if s == -AHEAD:
                    load_bases()
                    for c in range(DC // 2):
                        sum_bases(c)
                if s == NU - AHEAD:
                    for c in range(DC // 2, DC):
                        sum_bases(c)
                    low_part(wout_lo, wout_raw, wout_hi, wout_hi_ready, wout_ready)

            run_units(pool, unit_step)
            low_part(wffn_lo, wffn_sum, wffn_hi, wffn_hi_ready, wffn_ready)

            def output_step(s, it):
                t = s + 3
                if 0 <= t < TILES:
                    pool.wait_ge(o_loaded[t % 2], 2 * 16 * (t // 2 + 1) + 2 * 2 * 16 * it)
                    if t >= 2:
                        pool.wait_ge(att_lo_ready, t - 1 + 4 * it)
                    pool.tensor_tensor(att[t % 2][:], o_in[t % 2][:],
                                       inv_in[t % 2][:].rearrange("p (a t) -> p a t", a=1).broadcast_to([P, DC, P]),
                                       ALU.mult).then_inc(att_ready, 1)
                    pool.wait_ge(att_hi_ready, t + 1 + 4 * it)
                    pool.tensor_tensor(att_lo[t % 2][:], att[t % 2][:], att_hi[t % 2][:].bitcast(F32),
                                       ALU.subtract).then_inc(att_lo_ready, 1)

            run_outputs(pool, output_step)

        @block.scalar
        def _(act):
            def high_weights(i):
                act.wait_ge(wqkv_loaded[i], 16)
                for c in range(DC):
                    mine = slice(i * D, (i + 1) * D)
                    act.activation(wqkv_hi[:, c, mine], wqkv_raw[:, c, mine], ACT.Copy).then_inc(wqkv_hi_ready, 1)

            act.wait_ge(eps_ready, 1)

            def tile_step(s, it):
                if s == -1:
                    high_weights(0)
                if s == 0:
                    high_weights(1)
                    high_weights(2)
                t = s + 1
                if 0 <= t < TILES:
                    act.wait_ge(xt_done, t + 1 + 4 * it)
                    if t >= 2:
                        act.wait_ge(v_done, t - 1 + 4 * it)
                    act.activation(xt_hi[t % 2][:].rearrange("p c t -> p (c t)"), ps[:, XT_BANK, :],
                                   ACT.Copy).then_inc(xt_hi_ready, 1)
                t = s - 2
                half = ds((t % 2) * P, P)
                if 0 <= t < TILES:
                    act.wait_ge(qkt_done, t + 1 + 4 * it)
                    if t >= 4 and t % 2 == 0:
                        act.wait_ge(parts_stored[t // 2 % 2], 6 * 16 * (t // 4) + 6 * 16 * it)
                    act.activation(parts[t // 2 % 2][:, 0, :, :, half],
                                   ps[:, QKT_BANK:QKT_BANK + 2, :].rearrange("p i (c t) -> p i c t", c=DC),
                                   ACT.Copy).then_inc(hi_ready, 1)
                t = s + 2
                if 0 <= t < TILES:
                    act.wait_ge(x_var, t + 1 + 4 * it)
                    act.activation(x_sd[t % 2][:], x_mv[t % 2][:, 1:2], ACT.Sqrt, bias=eps[:]).then_inc(x_dev, 1)
                t = s - 2
                if 0 <= t < TILES:
                    act.wait_ge(rest_ready, t + 1 + 4 * it)
                    act.activation(parts[t // 2 % 2][:, 1, :, :, half], rest[:], ACT.Copy).then_inc(mid_ready, 1)
                t = s
                if 0 <= t < TILES:
                    act.wait_ge(qk_var, t + 1 + 4 * it)
                    act.activation(qk_sd[t % 2][:], qk_mv[t % 2][:, :, 1], ACT.Sqrt, bias=eps[:]).then_inc(qk_dev, 1)

            run_tiles(act, tile_step, -2, TILES + 1)

            def unit_step(s, it):
                if s == GROUPS * NU:
                    high_attention(0, 0)
                if s in WEIGHTS_AT:
                    c = WEIGHTS_AT.index(s)
                    if c == 0:
                        act.wait_ge(wout_loaded, 16)
                    if c < DC:
                        act.activation(wout_hi[:, c, :], wout_raw[:, c, :], ACT.Copy).then_inc(wout_hi_ready, 1)
                    else:
                        c -= DC
                        act.wait_ge(wffn_summed, 3 * (c + 1))
                        act.activation(wffn_hi[:, c, :], wffn_sum[:, c, :], ACT.Copy).then_inc(wffn_hi_ready, 1)
                for pair in range(2):
                    if 0 <= s < GROUPS * NU:
                        n = unit_columns(s % NU)[1]
                        act.wait_ge(scored, 2 * s + pair + 1 + 4 * NU * it)
                        if s >= P_SLOTS and pair == 0:
                            act.wait_ge(pv_done, s - P_SLOTS + 1 + 2 * NU * it)
                        act.activation(probs[s % P_SLOTS][:, 2 * pair:2 * pair + 2, 0:n],
                                       ps[:, EXP_BANK[pair]:EXP_BANK[pair] + 2, 0:n],
                                       ACT.Exp, scale=SCALE).then_inc(exp_done, 1)
                    last = s - LAG
                    if pair == 0 and last >= 0 and last % NU in (TPB // 2 - 1, NU - 1):
                        copy_half(last, it)
                    n = (s + AHEAD) // NU
                    if pair == 0 and (s + AHEAD) % NU == 0 and 0 <= n < GROUPS:
                        act.wait_ge(max_turned, n + 1 + 2 * it)
                        turned = ps[0:G * TPB, MAX_BANK + TURN_SLOT, 0:P]
                        act.activation(shift[n % 2][:], turned, ACT.Copy, scale=-1.0).then_inc(shift_hi_ready, 1)
                        act.activation(shift_hi[n % 2][:], turned, ACT.Copy, scale=-1.0).then_inc(shift_hi_ready, 1)

            def high_attention(t, it):
                act.wait_ge(att_ready, t + 1 + 4 * it)
                if t >= 2:
                    act.wait_ge(proj_done, t - 1 + 4 * it)
                act.activation(att_hi[t % 2][:], att[t % 2][:], ACT.Copy).then_inc(att_hi_ready, 1)

            def copy_half(u, it):
                half = 0 if u % NU == TPB // 2 - 1 else 1
                n = u // NU
                act.wait_ge(pv_done, u + 1 + 2 * NU * it)
                if n >= 1:
                    act.wait_ge(o_stored[half], 16 * n + 32 * it)
                act.activation(o_sb[half][:], ps[:, PV_BANK, :], ACT.Copy).then_inc(o_ready, 1)

            run_units(act, unit_step)

            def output_step(s, it):
                t = s + 3
                if 1 <= t < TILES:
                    high_attention(t, it)
                t = s + 2
                if 0 <= t < TILES:
                    act.wait_ge(y_var, t + 1 + 4 * it)
                    act.activation(y_sd[t % 2][:], y_mv[t % 2][:, 1:2], ACT.Sqrt, bias=eps[:]).then_inc(y_dev, 1)
                t = s + 1
                if 0 <= t < TILES:
                    act.wait_ge(yt_done, t + 1 + 4 * it)
                    if t >= 2:
                        act.wait_ge(ff_done, t - 1 + 4 * it)
                    act.activation(yt_hi[t % 2][:].rearrange("p c t -> p (c t)"), ps[:, YT_BANK[t % 2], :],
                                   ACT.Copy).then_inc(yt_hi_ready, 1)

            run_outputs(act, output_step)

        @block.vector
        def _(dve):
            def low_weights(i):
                for c in range(DC):
                    mine = slice(i * D, (i + 1) * D)
                    dve.wait_ge(wqkv_hi_ready, DC * i + c + 1)
                    dve.tensor_tensor(wqkv_lo[:, c, mine], wqkv_raw[:, c, mine], wqkv_hi[:, c, mine].bitcast(F32),
                                      ALU.subtract).then_inc(wqkv_ready, 1)

            def tile_step(s, it):
                if s == -1:
                    low_weights(0)
                if s == 0:
                    low_weights(1)
                    low_weights(2)
                t = s + 1
                if 0 <= t < TILES:
                    dve.wait_ge(xt_hi_ready, t + 1 + 4 * it)
                    dve.tensor_tensor(xt_lo[t % 2][:].rearrange("p c t -> p (c t)"), ps[:, XT_BANK, :],
                                      xt_hi[t % 2][:].bitcast(F32).rearrange("p c t -> p (c t)"),
                                      ALU.subtract).then_inc(xt_ready, 1)
                t = s + 2
                if 0 <= t < TILES:
                    dve.wait_ge(x_loaded[t % 2], 16 * (t // 2 + 1) + 32 * it)
                    dve.bn_stats(x_stat[:], x_in[t % 2][:]).then_inc(x_stats, 1)
                    wait_apart(dve, x_stats, t + 1 + 4 * it)
                    dve.bn_aggr(x_mv[t % 2][:], x_stat[:]).then_inc(x_var, 1)
                t = s - 2
                if 0 <= t < TILES:
                    dve.wait_ge(hi_ready, t + 1 + 4 * it)
                    if t >= 1:
                        dve.wait_ge(lo_ready, t + 4 * it)
                    dve.tensor_tensor(rest[:],
                                      ps[:, QKT_BANK:QKT_BANK + 2, :].rearrange("p i (c t) -> p i c t", c=DC),
                                      parts[t // 2 % 2][:, 0, :, :, ds((t % 2) * P, P)],
                                      ALU.subtract).then_inc(rest_ready, 1)
                t = s + 2
                if 0 <= t < TILES:
                    dve.wait_ge(x_dev, t + 1 + 4 * it)
                    dve.reciprocal(x_rs[t % 2][:], x_sd[t % 2][:]).then_inc(x_inv, 1)
                    dve.wait_ge(x_inv, t + 1 + 4 * it)
                    if t >= 2:
                        dve.wait_ge(xt_done, t - 1 + 4 * it)
                    dve.tensor_scalar(xn[t % 2][:], x_in[t % 2][:], x_mv[t % 2][:, 0:1], x_rs[t % 2][:],
                                      ALU.subtract, ALU.mult).then_inc(x_normed, 1)
                t = s
                if 0 <= t < TILES:
                    dve.wait_ge(qk_done, t + 1 + 4 * it)
                    if t >= 2:
                        dve.wait_ge(qkt_done, t - 1 + 4 * it)
                    bank = QK_BANK[t % 2]
                    dve.tensor_scalar(qk[t % 2][:], ps[:, bank:bank + 2, :], CLIP, -CLIP,
                                      ALU.min, ALU.max).then_inc(qk_clipped, 1)
                    dve.wait_ge(qk_clipped, t + 1 + 4 * it)
                    for i in range(2):
                        dve.bn_stats(qk_stat[:, i, :], qk[t % 2][:, i, :]).then_inc(qk_stats, 1)
                    wait_apart(dve, qk_stats, 2 * t + 2 + 8 * it)
                    dve.bn_aggr(qk_mv[t % 2][:, 0, :], qk_stat[:, 0, :])
                    dve.bn_aggr(qk_mv[t % 2][:, 1, :], qk_stat[:, 1, :]).then_inc(qk_var, 1)
                    dve.wait_ge(v_done, t + 1 + 4 * it)
                    if t == 0:
                        dve.wait_ge(ones_ready, 2)
                    if t >= 2:
                        dve.wait_ge(v_stored[t % 2], 16 * (t // 2) + 32 * it)
                    dve.tensor_scalar(v_ext[t % 2][:, :, 0:HD],
                                      ps[:, V_BANK, :].rearrange("p (h d) -> p h d", h=HEADS), CLIP, -CLIP,
                                      ALU.min, ALU.max).then_inc(v_clipped, 1)
                    dve.wait_ge(qk_dev, t + 1 + 4 * it)
                    dve.reciprocal(qk_rs[t % 2][:], qk_sd[t % 2][:]).then_inc(qk_inv, 1)
                    dve.wait_ge(qk_inv, t + 1 + 4 * it)
                    dve.tensor_scalar(qk[t % 2][:, 0, :], qk[t % 2][:, 0, :], qk_mv[t % 2][:, 0, 0:1],
                                      qk_rs[t % 2][:, 0:1], ALU.subtract, ALU.mult)
                    dve.tensor_scalar(qk[t % 2][:, 1, :], qk[t % 2][:, 1, :], qk_mv[t % 2][:, 1, 0:1],
                                      qk_rs[t % 2][:, 1:2], ALU.subtract, ALU.mult).then_inc(qk_normed, 1)

            def unit_step(s, it):
                n = (s + AHEAD) // NU
                if (s + AHEAD) % NU == 0 and 0 <= n < GROUPS:
                    dve.wait_ge(max_taken, NP * (n + 1) + 2 * NP * it)
                    late = max_diag[n % 2][:, :, TPB // 2:TPB]
                    dve.tensor_tensor(late, late, max_full[n % 2][:], ALU.max).then_inc(max_joined, 1)
                if s == (GROUPS - 1) * NU:
                    invert(0)
                v, n = (s + AHEAD) % NU, (s + AHEAD) // NU + 1
                if not 0 <= n < GROUPS:
                    return
                for m in sum(PLAN[v], []):
                    j, i, _, keys, diagonal = PIECES[m]
                    wait_apart(dve, max_scored, NP * n + m + 1 + 2 * NP * it)
                    scores = ps[:, MAX_BANK + m % MAX_RING, 0:keys]
                    if diagonal:
                        dve.tensor_tensor_reduce(max_junk[:, m % MAX_RING, 0:keys], scores, mask[:, BANK - keys:BANK], 1.0,
                                                 -3e38, ALU.add, ALU.max,
                                                 max_diag[n % 2][:, j, i:i + 1]).then_inc(max_taken, 1)
                    else:
                        i -= TPB // 2
                        dve.tensor_reduce(max_full[n % 2][:, j, i:i + 1], scores, AX.X,
                                          ALU.max).then_inc(max_taken, 1)

            def invert(b):
                dve.wait_ge(sums_loaded, 16 * (b + 1))
                dve.reciprocal(inv[:, b, :], sums[:, b, :]).then_inc(inverted, 1)

            run_tiles(dve, tile_step, -2, TILES)
            dve.wait_ge(mask_ready, 2)
            for s in range(FIRST_UNIT, FIRST_UNIT + EARLY_UNITS):
                unit_step(s, 0)
            tile_step(TILES + 1, 0)
            run_units(dve, unit_step, FIRST_UNIT + EARLY_UNITS)

            def output_step(s, it):
                if s == 0:
                    invert(1)
                t = s + 2
                if 0 <= t < TILES:
                    dve.wait_ge(proj_done, t + 1 + 4 * it)
                    dve.wait_ge(xr_loaded[t % 4], 16 * (t // 4 + 1) + 16 * it)
                    dve.tensor_tensor(x2[t % 4][:], ps[:, O_BANK[t % 2], :], x2[t % 4][:],
                                      ALU.add).then_inc(x2_ready, 1)
                    dve.wait_ge(x2_ready, t + 1 + 4 * it)
                    dve.bn_stats(y_stat[:], x2[t % 4][:]).then_inc(y_stats, 1)
                    wait_apart(dve, y_stats, t + 1 + 4 * it)
                    dve.bn_aggr(y_mv[t % 2][:], y_stat[:]).then_inc(y_var, 1)
                if 0 <= t < TILES:
                    dve.wait_ge(y_dev, t + 1 + 4 * it)
                    dve.reciprocal(y_rs[t % 2][:], y_sd[t % 2][:]).then_inc(y_inv, 1)
                    dve.wait_ge(y_inv, t + 1 + 4 * it)
                    if t >= 2:
                        dve.wait_ge(yt_done, t - 1 + 4 * it)
                    dve.tensor_scalar(yn[t % 2][:], x2[t % 4][:], y_mv[t % 2][:, 0:1], y_rs[t % 2][:],
                                      ALU.subtract, ALU.mult).then_inc(y_normed, 1)
                t = s + 1
                if 0 <= t < TILES:
                    dve.wait_ge(yt_hi_ready, t + 1 + 4 * it)
                    dve.tensor_tensor(yt_lo[t % 2][:].rearrange("p c t -> p (c t)"), ps[:, YT_BANK[t % 2], :],
                                      yt_hi[t % 2][:].bitcast(F32).rearrange("p c t -> p (c t)"),
                                      ALU.subtract).then_inc(yt_ready, 1)
                t = s
                if 0 <= t < TILES:
                    dve.wait_ge(ff_done, t + 1 + 4 * it)
                    if t >= 2:
                        dve.wait_ge(y_stored[t % 2], 16 * (t // 2) + 32 * it)
                    dve.tensor_tensor(y_out[t % 2][:], ps[:, FF_BANK[t % 2], :], x2[t % 4][:],
                                      ALU.add).then_inc(y_ready, 1)

            run_outputs(dve, output_step)

        @block.tensor
        def _(pe):
            def product(to, hi, lo, w_hi, w_lo):
                for c in range(DC):
                    pe.matmul(to, hi[:, c, :], w_hi[:, c, :], start=(c == 0), stop=False)
                    pe.matmul(to, hi[:, c, :], w_lo[:, c, :], start=False, stop=False)
                    last = pe.matmul(to, lo[:, c, :], w_hi[:, c, :], start=False, stop=(c == DC - 1))
                return last

            def turn(bank, rows):
                for c in range(DC):
                    last = pe.transpose(ps[:, bank, c * P:(c + 1) * P], rows[:, c * P:(c + 1) * P], ident[:])
                return last

            pe.wait_ge(ident_ready, 2)

            def tile_step(s, it):
                t = s + 1
                if 0 <= t < TILES:
                    pe.wait_ge(x_normed, t + 1 + 4 * it)
                    if t >= 1:
                        pe.wait_ge(xt_ready, t + 4 * it)
                    turn(XT_BANK, xn[t % 2]).then_inc(xt_done, 1)
                t = s
                if 0 <= t < TILES:
                    pe.wait_ge(xt_ready, t + 1 + 4 * it)
                    if t >= 2:
                        pe.wait_ge(qk_clipped, t - 1 + 4 * it)
                    for i in range(2):
                        if t == 0:
                            pe.wait_ge(wqkv_ready, DC * (i + 1))
                        last = product(ps[:, QK_BANK[t % 2] + i, :], xt_hi[t % 2], xt_lo[t % 2],
                                       wqkv_hi[:, :, i * D:(i + 1) * D], wqkv_lo[:, :, i * D:(i + 1) * D])
                    last.then_inc(qk_done, 1)
                    if t == 0:
                        pe.wait_ge(wqkv_ready, DC * 3)
                    if t >= 1:
                        pe.wait_ge(v_clipped, t + 4 * it)
                    product(ps[:, V_BANK, :], xt_hi[t % 2], xt_lo[t % 2],
                            wqkv_hi[:, :, 2 * D:3 * D], wqkv_lo[:, :, 2 * D:3 * D]).then_inc(v_done, 1)
                t = s - 1
                if 0 <= t < TILES:
                    pe.wait_ge(qk_ready, t + 1 + 4 * it)
                    if t >= 1:
                        pe.wait_ge(rest_ready, t + 4 * it)
                    turn(QKT_BANK, qk[t % 2][:, 0, :])
                    turn(QKT_BANK + 1, qk[t % 2][:, 1, :]).then_inc(qkt_done, 1)

            def unit_step(s, it):
                v, n_max = (s + AHEAD) % NU, (s + AHEAD) // NU + 1

                def max_pieces_of(slot):
                    if not 0 <= n_max < GROUPS:
                        return
                    for m in PLAN[v][slot]:
                        j, i, key, keys, _ = PIECES[m]
                        if m == 0 and n_max == 0:
                            pe.wait_ge(qk_clipped, TILES - 1)
                        if m == 0:
                            pe.wait_ge(max_loaded[n_max % 2], 128 * (n_max // 2 + 1) + 128 * it)
                        if m == TURN_SLOT and n_max >= 1:
                            pe.wait_ge(shift_hi_ready, 2 * n_max + 4 * it)
                        if NP * n_max + m >= MAX_RING:
                            pe.wait_ge(max_taken, NP * n_max + m - MAX_RING + 1 + 2 * NP * it)
                        rows = MAX_K + BIAS_ROWS
                        pe.matmul(ps[:, MAX_BANK + m % MAX_RING, 0:keys],
                                  max_q[n_max % 2][0:rows, j, i * P:(i + 1) * P],
                                  max_k[n_max % 2][0:rows, j, key:key + keys],
                                  start=True, stop=True).then_inc(max_scored, 1)

                def score(pair):
                    u, n = s % NU, s // NU
                    first_q, cols = unit_columns(u)
                    kb = UNITS[u][1]
                    rows = EXP_K + BIAS_ROWS + SHIFT_ROWS
                    if u == 0 and pair == 0:
                        pe.wait_ge(exp_loaded[n % 2], 224 * (n // 2 + 1) + 224 * it)
                        pe.wait_ge(shift_loaded[n % 2], 32 * (n // 2 + 1) + 32 * it)
                    if s >= 1:
                        pe.wait_ge(exp_done, 2 * s - 1 + pair + 4 * NU * it)
                    for j in range(2):
                        last = pe.matmul(ps[:, EXP_BANK[pair] + j, 0:cols],
                                         exp_k[n % 2][0:rows, 2 * pair + j, kb * P:(kb + 1) * P],
                                         exp_q[n % 2][0:rows, 2 * pair + j, first_q:first_q + cols],
                                         start=True, stop=not is_diagonal(u))
                        if is_diagonal(u):
                            last = pe.matmul(ps[:, EXP_BANK[pair] + j, 0:P], ident_half[:], mask_turned[:],
                                             start=False, stop=True)
                    last.then_inc(scored, 1)

                if s == 0:
                    pe.wait_ge(mask_ready, 2)
                    pe.wait_ge(rest_ready, TILES)
                    pe.wait_ge(v_clipped, TILES)
                if 0 <= s < GROUPS * NU:
                    score(0)
                max_pieces_of(0)
                w = s - LAG
                if 0 <= w < GROUPS * NU:
                    u, n = w % NU, w // NU
                    half, kb = UNITS[u]
                    first_q, cols = unit_columns(u)
                    if u == 0:
                        pe.wait_ge(v_loaded[n % 2], 16 * (n // 2 + 1) + 16 * it)
                    if kb == 0 and 2 * n + half >= 1:
                        pe.wait_ge(o_ready, 2 * n + half + 4 * it)
                    pe.wait_ge(exp_done, 2 * (w + 1) + 4 * NU * it)
                    to = first_q - half * BANK
                    last_kb = (half + 1) * TPB // 2 - 1
                    for j in range(G):
                        last = pe.matmul(ps[j * VW:(j + 1) * VW, PV_BANK, to:to + cols],
                                         v_sb[n % 2][:, kb, j * VW:(j + 1) * VW],
                                         probs[w % P_SLOTS][:, j, 0:cols],
                                         start=(kb == 0), stop=(kb == last_kb))
                    last.then_inc(pv_done, 1)
                max_pieces_of(1)
                n = n_max - 1
                if v == 0 and 0 <= n < GROUPS:
                    pe.wait_ge(max_joined, n + 1 + 2 * it)
                    pe.transpose(ps[0:G * TPB, MAX_BANK + TURN_SLOT, 0:P],
                                 max_diag[n % 2][:].rearrange("p j i -> p (j i)"), ident[:]).then_inc(max_turned, 1)
                if 0 <= s < GROUPS * NU:
                    score(1)
                max_pieces_of(2)

            run_tiles(pe, tile_step, -1, TILES - 1)
            for s in range(FIRST_UNIT, FIRST_UNIT + EARLY_UNITS):
                unit_step(s, 0)
            tile_step(TILES, 0)
            run_units(pe, unit_step, FIRST_UNIT + EARLY_UNITS)
            pe.wait_ge(o_ready, 2 * GROUPS)

            def output_step(s, it):
                t = s + 2
                if 0 <= t < TILES:
                    if t == 0:
                        pe.wait_ge(wout_ready, DC)
                    pe.wait_ge(att_lo_ready, t + 1 + 4 * it)
                    if t >= 2:
                        pe.wait_ge(x2_ready, t - 1 + 4 * it)
                    product(ps[:, O_BANK[t % 2], :], att_hi[t % 2], att_lo[t % 2],
                            wout_hi, wout_lo).then_inc(proj_done, 1)
                t = s + 1
                if 0 <= t < TILES:
                    pe.wait_ge(y_normed, t + 1 + 4 * it)
                    if t >= 2:
                        pe.wait_ge(yt_ready, t - 1 + 4 * it)
                    turn(YT_BANK[t % 2], yn[t % 2]).then_inc(yt_done, 1)
                t = s
                if 0 <= t < TILES:
                    if t == 0:
                        pe.wait_ge(wffn_ready, DC)
                    pe.wait_ge(yt_ready, t + 1 + 4 * it)
                    if t >= 2:
                        pe.wait_ge(y_ready, t - 1 + 4 * it)
                    product(ps[:, FF_BANK[t % 2], :], yt_hi[t % 2], yt_lo[t % 2],
                            wffn_hi, wffn_lo).then_inc(ff_done, 1)

            run_outputs(pe, output_step)


def alibi_rows(bf16):
    steps = np.arange(1, HEADS + 1, dtype=np.float32) * (ALIBI_MAX / HEADS)
    slopes = (1.0 / np.power(2.0, steps)).astype(np.float32)
    bias = slopes[:, None].astype(np.float64) * np.arange(SEQ) / SCALE
    rows = np.ones((2, BIAS_ROWS + SHIFT_ROWS, HEADS, SEQ), dtype=bf16)
    for n in range(3):
        part = bias.astype(np.float32).astype(bf16)
        bias = bias - part.astype(np.float64)
        rows[1, 2 * n] = part
        rows[0, 2 * n + 1] = -part
    return rows


def kernel(L0_attn_hidden_states, L0_attn_Wqkv, L0_attn_q_ln_w, L0_attn_q_ln_b, L0_attn_k_ln_w,
           L0_attn_k_ln_b, L0_attn_Wout, L0_ffn_bases, L0_ffn_alphas):
    import ml_dtypes
    import concourse.bacc as bacc
    from concourse.bass_utils import run_bass_kernel_spmd

    x = np.asarray(L0_attn_hidden_states)
    arrays = {
        "x": np.ascontiguousarray(x.reshape(TILES, P, D)),
        "wqkv_t": np.ascontiguousarray(np.asarray(L0_attn_Wqkv).T),
        "qk_w": np.stack([np.asarray(L0_attn_q_ln_w), np.asarray(L0_attn_k_ln_w)]),
        "qk_b": np.stack([np.asarray(L0_attn_q_ln_b), np.asarray(L0_attn_k_ln_b)]),
        "wout_t": np.ascontiguousarray(np.asarray(L0_attn_Wout).reshape(D, HEADS, HD).transpose(2, 1, 0).reshape(D, D)),
        "bases_t": np.ascontiguousarray(np.asarray(L0_ffn_bases).transpose(0, 2, 1)),
        "alphas": np.ascontiguousarray(np.asarray(L0_ffn_alphas)[:, :, 0]),
        "bias_rows": alibi_rows(ml_dtypes.bfloat16),
    }
    nc = bacc.Bacc("TRN2", target_bir_lowering=False, num_devices=1)
    args = [nc.dram_tensor(f"in_{k}", a.shape, mybir.dt.from_np(a.dtype), kind="ExternalInput").ap()
            for k, a in arrays.items()]
    out = nc.dram_tensor("out", (TILES, P, D), F32, kind="ExternalOutput").ap()
    build(nc, *args, out)
    r = run_bass_kernel_spmd(nc, [{f"in_{k}": a for k, a in arrays.items()}], core_ids=[0])
    return r.results[0]["out"].reshape(x.shape)
```
